# Optimizing a Trainium2 kernel written in Bass

```python
import numpy as np
import jax
import jax.numpy as jnp

def _softmax(x, axis=-1):
    return jax.nn.softmax(x, axis=axis)

def _gelu(x):
    return jax.nn.gelu(x, approximate=True)

def _silu(x):
    return jax.nn.silu(x)

def _sigmoid(x):
    return jax.nn.sigmoid(x)

def _layernorm(x, axis=-1, eps=1e-05):
    m = jnp.mean(x, axis=axis, keepdims=True)
    v = jnp.var(x, axis=axis, keepdims=True)
    return (x - m) / jnp.sqrt(v + eps)

def _scatter_add(tgt, idx, src, axis=0):
    return tgt.at[idx].add(src)

def _segment_sum(src, seg, n):
    return jax.ops.segment_sum(src, seg, n)
kernel_name = 'mk_seq_preln_d1_jaxref_r8_30298d'

def setup_inputs(seed: int=0):
    np.random.seed(seed)
    _w = jnp.asarray

    def _L0_attn_setup():
        import jax, jax.numpy as jnp
        import numpy as np
        D_MODEL = 128
        N_HEADS = 16
        D_HEAD = D_MODEL // N_HEADS
        B, L = (2, 256)
        key = jax.random.key(seed)
        ks = jax.random.split(key, 9)
        s = 1.0 / np.sqrt(D_MODEL)
        inp = {'x': jax.random.normal(ks[0], (B, L, D_MODEL), dtype=jnp.float32)}
        for i, name in enumerate(['wq', 'wk', 'wv', 'wo']):
            inp[name + '_w'] = jax.random.normal(ks[1 + 2 * i], (D_MODEL, D_MODEL), dtype=jnp.float32) * s
            inp[name + '_b'] = jax.random.normal(ks[2 + 2 * i], (D_MODEL,), dtype=jnp.float32) * 0.01
        return inp
    _L0_attn_in = _L0_attn_setup()

    def _L0_ffn_setup():
        import jax, jax.numpy as jnp
        import numpy as np
        NUM_EXPERTS = 8
        TOP_K = 2
        key = jax.random.key(seed)
        ks = jax.random.split(key, 6)
        B, S, D, H, E = (4, 128, 128, 256, NUM_EXPERTS)
        x = jax.random.normal(ks[0], (B, S, D), dtype=jnp.float32)
        Wg = jax.random.normal(ks[1], (D, E), dtype=jnp.float32) * 0.02
        W1 = jax.random.normal(ks[2], (E, D, H), dtype=jnp.float32) * 0.02
        b1 = jax.random.normal(ks[3], (E, H), dtype=jnp.float32) * 0.02
        W2 = jax.random.normal(ks[4], (E, H, D), dtype=jnp.float32) * 0.02
        b2 = jax.random.normal(ks[5], (E, D), dtype=jnp.float32) * 0.02
        return {'x': x, 'Wg': Wg, 'W1': W1, 'b1': b1, 'W2': W2, 'b2': b2}
    _L0_ffn_in = _L0_ffn_setup()
    _d = {'L0_attn_x': _L0_attn_in['x'], 'L0_attn_wq_w': _L0_attn_in['wq_w'], 'L0_attn_wq_b': _L0_attn_in['wq_b'], 'L0_attn_wk_w': _L0_attn_in['wk_w'], 'L0_attn_wk_b': _L0_attn_in['wk_b'], 'L0_attn_wv_w': _L0_attn_in['wv_w'], 'L0_attn_wv_b': _L0_attn_in['wv_b'], 'L0_attn_wo_w': _L0_attn_in['wo_w'], 'L0_attn_wo_b': _L0_attn_in['wo_b'], 'L0_ffn_Wg': _L0_ffn_in['Wg'], 'L0_ffn_W1': _L0_ffn_in['W1'], 'L0_ffn_b1': _L0_ffn_in['b1'], 'L0_ffn_W2': _L0_ffn_in['W2'], 'L0_ffn_b2': _L0_ffn_in['b2']}
    _x0 = _d['L0_attn_x']
    _d['L0_attn_x'] = jax.random.normal(jax.random.fold_in(jax.random.key(seed), 1), (8, 512, 128), dtype=_x0.dtype)
    del _x0
    return _d

def reference(L0_attn_x, L0_attn_wq_w, L0_attn_wq_b, L0_attn_wk_w, L0_attn_wk_b, L0_attn_wv_w, L0_attn_wv_b, L0_attn_wo_w, L0_attn_wo_b, L0_ffn_Wg, L0_ffn_W1, L0_ffn_b1, L0_ffn_W2, L0_ffn_b2):

    def _L0_attn_ref(x, wq_w, wq_b, wk_w, wk_b, wv_w, wv_b, wo_w, wo_b):
        import jax, jax.numpy as jnp
        import numpy as np
        D_MODEL = 128
        N_HEADS = 16
        D_HEAD = D_MODEL // N_HEADS
        B, L = (2, 256)
        b, l, d = x.shape
        h, dh = (N_HEADS, D_HEAD)

        def proj(w, bias):
            return (jnp.einsum('bld,ed->ble', x, w) + bias).reshape(b, l, h, dh).transpose(0, 2, 1, 3)
        Q, K, V = (proj(wq_w, wq_b), proj(wk_w, wk_b), proj(wv_w, wv_b))
        scores = jnp.einsum('bhld,bhsd->bhls', Q, K)
        causal = jnp.tril(jnp.ones((l, l), dtype=scores.dtype))
        out = jnp.einsum('bhls,bhsd->bhld', scores * causal, V)
        out = out.transpose(0, 2, 1, 3).reshape(b, l, d)
        return jnp.einsum('bld,ed->ble', out, wo_w) + wo_b

    def _L0_ffn_ref(x, Wg, W1, b1, W2, b2):
        import jax, jax.numpy as jnp
        import numpy as np
        NUM_EXPERTS = 8
        TOP_K = 2
        B, S, D = x.shape
        E, _, H = W1.shape
        OUT = W2.shape[2]
        xm = x.reshape(-1, D)
        logits = xm @ Wg
        probs = jax.nn.softmax(logits, axis=-1)
        topk_p, topk_i = jax.lax.top_k(probs, TOP_K)
        flat_e = topk_i.reshape(-1)
        flat_p = topk_p.reshape(-1)
        order = jnp.argsort(flat_e)
        tok_idx = order // TOP_K
        e_sorted = flat_e[order]
        p_sorted = flat_p[order]
        xs = xm[tok_idx]
        y = jnp.zeros((xs.shape[0], OUT), dtype=xs.dtype)
        for e in range(E):
            h = jax.nn.relu(xs @ W1[e] + b1[e])
            ye = h @ W2[e] + b2[e]
            m = (e_sorted == e)[:, None].astype(xs.dtype)
            y = y + m * ye
        y = y * p_sorted[:, None]
        out = jnp.zeros((B * S, OUT), dtype=y.dtype).at[tok_idx].add(y)
        return out.reshape(B, S, OUT)
    x = L0_attn_x
    x = x + _L0_attn_ref(_layernorm(x, axis=-1), L0_attn_wq_w, L0_attn_wq_b, L0_attn_wk_w, L0_attn_wk_b, L0_attn_wv_w, L0_attn_wv_b, L0_attn_wo_w, L0_attn_wo_b)
    x = x + _L0_ffn_ref(_layernorm(x, axis=-1), L0_ffn_Wg, L0_ffn_W1, L0_ffn_b1, L0_ffn_W2, L0_ffn_b2)
    return x

_drawn_inputs = setup_inputs


def setup_inputs(seed=0):
    import zlib

    import numpy as np

    out = dict(_drawn_inputs(seed))
    spreads = {}
    factors = {'L0_attn_wq_b': 5.877,
     'L0_attn_wk_b': 8.0,
     'L0_attn_wv_b': 8.0,
     'L0_attn_wo_b': 200.0,
     'L0_ffn_Wg': 21.42,
     'L0_ffn_W1': 24.238,
     'L0_ffn_b1': 178.831,
     'L0_ffn_W2': 8.0,
     'L0_ffn_b2': 200.0}
    for name, (base, spread) in spreads.items():
        noise = np.random.default_rng([zlib.crc32(name.encode()), seed]).standard_normal(out[name].shape)
        drawn = base * np.exp(spread * noise) if base else spread * noise
        out[name] = jnp.asarray(drawn.astype(out[name].dtype))
    for name, factor in factors.items():
        out[name] = (out[name] * factor).astype(out[name].dtype)
    return out
```

```python
from contextlib import ExitStack

import concourse.bass as bass
from concourse import mybir

ALU = mybir.AluOpType
ACT = mybir.ActivationFunctionType
AX_X = mybir.AxisListType.X
F32 = mybir.dt.float32
BF16 = mybir.dt.bfloat16
I32 = mybir.dt.int32
U32 = mybir.dt.uint32

P = 128
HEADS = 16
DH = P // HEADS
EPS = 1e-5


def wait(eng, sem, value, most=None):
    if isinstance(value, int):
        value = value if most is None else min(value, most)
        if value <= 0:
            return
    eng.wait_ge(sem, value)


def run_slots(eng, stages, n_tiles, group):
    deepest = max(lag for lag, _ in stages)
    first = -(-deepest // group) * group + group
    for s in range(first):
        for lag, stage in stages:
            if s >= lag:
                stage((s - lag) // group, (s - lag) % group)
    with eng.Fori(first // group, n_tiles // group) as i:
        for t in range(group):
            for lag, stage in stages:
                stage(i + (t - lag) // group, (t - lag) % group)
    for s in range(n_tiles, n_tiles + deepest):
        for lag, stage in stages:
            if s - lag < n_tiles:
                stage((s - lag) // group, (s - lag) % group)


def preln_linear_attention_moe(nc, x, w_qkv, b_qkv, b_q, w_o, b_o, w_gate, w1, b1, w2, b2, out):
    B, L, D = x.shape
    E, _, H = w1.shape
    T = L // P
    N = B * T
    TOKENS = N * P
    HC = H // P
    OUTER = D * DH
    K = 2
    ROW = D + 4
    REGION = TOKENS + P
    PAD_BLOCK = E * REGION
    NOWHERE = K * TOKENS
    G = 8
    BLOCKS = -(-((K * TOKENS + E * (P - 1)) // P) // G) * G
    assert D == P and T == 4 and H == HC * P

    with ExitStack() as ctx:
        def sb(name, shape, dt=F32):
            return ctx.enter_context(nc.sbuf_tensor(name, shape, dt))

        def sem(name):
            return ctx.enter_context(nc.semaphore(name))

        dispatched = nc.dram_tensor("dispatched", [PAD_BLOCK + P, ROW], F32, kind="Internal").ap()
        returned = nc.dram_tensor("returned", [K * TOKENS, D], F32, kind="Internal").ap()

        ident = sb("ident", [P, P])
        causal = sb("causal", [P, P])
        earlier = sb("earlier", [P, P], BF16)
        ones = sb("ones", [P, P], BF16)
        headmask = sb("headmask", [P, P])
        neghalf = sb("neghalf", [P, 1])
        expert_no = sb("expert_no", [P, E])
        region_of = sb("region_of", [P, E])
        block_no = sb("block_no", [1, BLOCKS])
        block_row = sb("block_row", [1, BLOCKS])
        padding = sb("padding", [P, ROW])
        wqkv_sb = sb("wqkv_sb", [P, 3 * D])
        bqkv_bc = sb("bqkv_bc", [P, 3 * D])
        bq_col = sb("bq_col", [P, 1])
        wo_sb = sb("wo_sb", [P, D])
        bo_bc = sb("bo_bc", [P, D])
        wg_sb = sb("wg_sb", [P, E])
        w1_sb = sb("w1_sb", [P, E * H])
        b1_bc = sb("b1_bc", [P, E * H])
        w2_sb = sb("w2_sb", [P, HC, E * D])
        b2_bc = sb("b2_bc", [P, E * D])
        x_sb = sb("x_sb", [P, N * D])
        x2_sb = sb("x2_sb", [P, N * D])
        back = sb("back", [P, N * K * D])
        chosen = sb("chosen", [P, N * K])
        stats = sb("stats", [P, T, 6])
        mv = sb("mv", [P, T, 2])
        norm = sb("norm", [P, T, 2])
        xn = sb("xn", [P, T, D])
        xnT = sb("xnT", [P, T, P])
        qT = sb("qT", [P, T, P])
        qkv = sb("qkv", [P, T, 3 * D])
        outer = sb("outer", [P, T, OUTER])
        state = sb("state", [P, T, D])
        prod = sb("prod", [P, 2, OUTER])
        o_sb = sb("o_sb", [P, T, D])
        oT = sb("oT", [P, T, P])
        xb = sb("xb", [P, T, D])
        stats2 = sb("stats2", [P, T, 6])
        mv2 = sb("mv2", [P, T, 2])
        norm2_part = sb("norm2_part", [P, T, 2])
        norm2 = sb("norm2", [P, N * 2])
        xn2 = sb("xn2", [P, T, D])
        rows = sb("rows", [P, T, K, ROW])
        xn2T = sb("xn2T", [P, T, P])
        gmax = sb("gmax", [P, T])
        shifted = sb("shifted", [P, T, E])
        expd = sb("expd", [P, T, E])
        gsum = sb("gsum", [P, T])
        grec = sb("grec", [P, T])
        top = sb("top", [P, T, E])
        top_i = sb("top_i", [P, T, E], U32)
        top_f = sb("top_f", [P, T, K])
        pick = sb("pick", [P, T, K, E])
        picked = sb("picked", [P, T, E], BF16)
        picked_sum = sb("picked_sum", [P, E])
        picked_before = sb("picked_before", [P, E])
        picked_before_h = sb("picked_before_h", [P, E], BF16)
        place = sb("place", [P, T, E])
        place_of = sb("place_of", [P, T, K, E])
        slot_f = sb("slot_f", [P, T, K])
        slot_next = sb("slot_next", [P, T * K], I32)
        slot = sb("slot", [P, T * K], I32)
        cnt = sb("cnt", [1, E])
        cnt_i = sb("cnt_i", [1, E], I32)
        end_row_f = sb("end_row_f", [1, E])
        end_row = sb("end_row", [1, E], I32)
        n_blocks = sb("n_blocks", [1, E])
        one_row = sb("one_row", [1, E])
        end_block = sb("end_block", [1, E])
        jump = sb("jump", [1, E])
        past = sb("past", [1, BLOCKS, E])
        skipped = sb("skipped", [1, BLOCKS, E])
        blk = sb("blk", [1, BLOCKS, 2])
        table_f = sb("table_f", [1, BLOCKS, 4])
        table = sb("table", [1, BLOCKS * 4], I32)
        xt = sb("xt", [P, G, ROW])
        xT = sb("xT", [P, G, P])
        z_sb = sb("z_sb", [P, G, H])
        hT = sb("hT", [P, G, HC, P])
        y_sb = sb("y_sb", [P, G, D])

        ps = ctx.enter_context(nc.psum_tensor("ps", [P, 8, 512], F32))
        ps_T1 = ps[:, 0, 0:P]
        ps_oT = ps[:, 0, P:2 * P]
        ps_qT = ps[:, 1, 0:P]
        ps_T2 = ps[:, 1, P:2 * P]
        ps_run = [ps[:, 2:4, :], ps[:, 4:6, :]]
        ps_qkv = ps[:, 6, 0:3 * D]
        ps_state = ps[:, 7, 0:D]
        ps_att = ps[:, 7, P:2 * P]
        ps_lg = ps[:, 7, 2 * P:2 * P + T * E].rearrange("p (t e) -> p t e", t=T)
        ps_place = ps[:, 7, 3 * P:3 * P + T * E].rearrange("p (t e) -> p t e", t=T)
        ps_cnt = ps[0:1, 7, 3 * P + T * E:3 * P + T * E + E]
        ps_x = [ps[:, u, 0:P] for u in range(2)]
        ps_z = [ps[:, 2 + u, 0:H] for u in range(2)]
        ps_h = [ps[:, 4 + u, 0:H] for u in range(2)]
        ps_y = [ps[:, 6 + u, 0:D] for u in range(2)]

        consts, passed = sem("consts"), sem("passed")
        x_first, x_rest = sem("x_first"), sem("x_rest")
        w_att, w_ffn = sem("w_att"), sem("w_ffn")
        stats_raw, stats_done, norm_half, norm_done = sem("stats_raw"), sem("stats_done"), sem("norm_half"), sem("norm_done")
        xn_done, T1_done, xnT_done = sem("xn_done"), sem("T1_done"), sem("xnT_done")
        qkv_mm, qT_done, qkv_done = sem("qkv_mm"), sem("qT_done"), sem("qkv_done")
        outer_done, run_done, kv_done, state_done = sem("outer_done"), sem("run_done"), sem("kv_done"), sem("state_done")
        prod_done, o_done, oT_mm, oT_done = sem("prod_done"), sem("o_done"), sem("oT_mm"), sem("oT_done")
        att_mm, xb_done, x2_done = sem("att_mm"), sem("xb_done"), sem("x2_done")
        stats2_raw, stats2_done, norm2_half, norm2_done = sem("stats2_raw"), sem("stats2_done"), sem("norm2_half"), sem("norm2_done")
        xn2_done, rows_done, T2_done, xn2T_done = sem("xn2_done"), sem("rows_done"), sem("T2_done"), sem("xn2T_done")
        lg_mm = sem("lg_mm")
        gmax_done, shift_done, exp_done, gsum_done = sem("gmax_done"), sem("shift_done"), sem("exp_done"), sem("gsum_done")
        grec_done, top_done, topi_done, topf_done = sem("grec_done"), sem("top_done"), sem("topi_done"), sem("topf_done")
        chosen_done, pick_done, picked_done, place_mm = sem("chosen_done"), sem("pick_done"), sem("picked_done"), sem("place_mm")
        psum_done, before_done, before_h_done = sem("psum_done"), sem("before_done"), sem("before_h_done")
        place_done, placeof_done, slotf_done, slot_done = sem("place_done"), sem("placeof_done"), sem("slotf_done"), sem("slot_done")
        slots_taken = sem("slots_taken")
        dispatch_done = [sem(f"dispatch_done{t}") for t in range(T)]
        cnt_mm, table_step, end_row_done, table_done, pads_done = sem("cnt_mm"), sem("table_step"), sem("end_row_done"), sem("table_done"), sem("pads_done")
        xt_in = [sem(f"xt_in{t}") for t in range(G)]
        TX_done, xT_done, z_mm, z_done, TH_done, hT_done, y_mm, y_done = (
            sem("TX_done"), sem("xT_done"), sem("z_mm"), sem("z_done"), sem("TH_done"), sem("hT_done"), sem("y_mm"), sem("y_done"))
        dest_moved = sem("dest_moved")
        return_done = [sem(f"return_done{t}") for t in range(G)]
        back_in = [sem(f"back_in{b}") for b in range(B)]
        first_added, both_added = sem("first_added"), sem("both_added")
        stored = sem("stored")

        def tile(buf, b, t):
            return buf[:, bass.ds((T * b + t) * P, P)]

        def norm2_at(b, t, w):
            return norm2[:, bass.ds((T * b + t) * 2 + w, 1)]

        def bcast(ap):
            return ap.partition_broadcast(P)

        x_t = x.rearrange("b (t p) d -> b p t d", p=P)
        out_t = out.rearrange("b (t p) d -> b p t d", p=P)
        back_t = returned.rearrange("(b t p k) d -> b p t (k d)", b=B, t=T, k=K)

        N_FILLS = 12
        N_CONSTS = N_FILLS + 10
        block = ctx.enter_context(nc.Block())

        def apart(eng):
            eng.sem_inc(passed, 1)

        @block.sync
        def _(sp):
            def load_x(b):
                return sp.dma_start(x_sb[:, b * T * D:(b + 1) * T * D].rearrange("p (t d) -> p t d", t=T), x_t[b])
            load_x(0).then_inc(x_first, 16)
            sp.dma_start(wqkv_sb[:, :], w_qkv).then_inc(w_att, 16)
            sp.dma_start(bqkv_bc[:, :], bcast(b_qkv)).then_inc(w_att, 16)
            sp.dma_start(bq_col[:, :], b_q).then_inc(w_att, 16)
            sp.dma_start(wo_sb[:, :], w_o).then_inc(w_att, 16)
            sp.dma_start(bo_bc[:, :], bcast(b_o)).then_inc(w_att, 16)
            sp.dma_start(wg_sb[:, :], w_gate).then_inc(w_att, 16)
            for b in range(1, B):
                load_x(b).then_inc(x_rest, 16)
            sp.dma_start(w1_sb[:, :].rearrange("d (e h) -> d e h", e=E), w1.rearrange("e d h -> d e h")).then_inc(w_ffn, 16)
            sp.dma_start(b1_bc[:, :], bcast(b1)).then_inc(w_ffn, 16)
            for c in range(HC):
                sp.dma_start(w2_sb[:, c, :].rearrange("p (e d) -> p e d", e=E),
                             w2[:, c * P:(c + 1) * P, :].rearrange("e p d -> p e d")).then_inc(w_ffn, 16)
            sp.dma_start(b2_bc[:, :], bcast(b2)).then_inc(w_ffn, 16)
            sp.wait_ge(consts, N_CONSTS)
            sp.dma_start(dispatched[PAD_BLOCK:PAD_BLOCK + P, :], padding[:, :]).then_inc(pads_done, 16)

            sp.wait_ge(end_row_done, 1)
            for e in range(E):
                row = sp.value_load(end_row[0:1, e:e + 1], min_val=e * REGION, max_val=e * REGION + TOKENS)
                sp.dma_start(dispatched[bass.ds(row, P), :], padding[:, :]).then_inc(pads_done, 16)
            sp.wait_ge(table_done, 1)
            sp.wait_ge(pads_done, 16 * (E + 1))
            for t in range(T):
                sp.wait_ge(dispatch_done[t], 16 * B * K)

            def load_block(i, t):
                wait(sp, TX_done, G * (i - 1) + t + 1)
                apart(sp)
                wait(sp, return_done[t], 16 * i)
                apart(sp)
                row = sp.value_load(table[0:1, bass.ds((G * i + t) * 4, 1)], min_val=0, max_val=PAD_BLOCK)
                sp.dma_start(xt[:, t, :], dispatched[bass.ds(row, P), :]).then_inc(xt_in[t], 16)

            for t in range(G):
                load_block(0, t)
            with sp.Fori(1, BLOCKS // G) as i:
                for t in range(G):
                    load_block(i, t)

            for t in range(G):
                sp.wait_ge(return_done[t], 16 * (BLOCKS // G))
            for b in range(B):
                sp.dma_start(back[:, b * T * K * D:(b + 1) * T * K * D].rearrange("p (t f) -> p t f", t=T),
                             back_t[b]).then_inc(back_in[b], 16)
            for b in range(B):
                sp.wait_ge(both_added, (b + 1) * T)
                sp.dma_start(out_t[b], x2_sb[:, b * T * D:(b + 1) * T * D].rearrange("p (t d) -> p t d", t=T)).then_inc(stored, 16)
            sp.wait_ge(stored, 16 * B)

        @block.gpsimd
        def _(pool):
            pool.memset(ident[:, :], 0.0).then_inc(consts, 1)
            pool.memset(causal[:, :], 1.0).then_inc(consts, 1)
            pool.memset(earlier[:, :], 1.0).then_inc(consts, 1)
            pool.memset(ones[:, :], 1.0).then_inc(consts, 1)
            pool.memset(headmask[:, :], 1.0).then_inc(consts, 1)
            pool.memset(neghalf[:, :], -0.5).then_inc(consts, 1)
            pool.memset(padding[:, :], 0.0).then_inc(consts, 1)
            pool.memset(picked_before[:, :], 0.0).then_inc(consts, 1)
            pool.iota(expert_no[:, :], pattern=[[1, E]], base=0, channel_multiplier=0,
                      allow_small_or_imprecise_dtypes=True).then_inc(consts, 1)
            pool.iota(region_of[:, :], pattern=[[REGION, E]], base=0, channel_multiplier=0,
                      allow_small_or_imprecise_dtypes=True).then_inc(consts, 1)
            pool.iota(block_no[:, :], pattern=[[1, BLOCKS]], base=0, channel_multiplier=0,
                      allow_small_or_imprecise_dtypes=True).then_inc(consts, 1)
            pool.iota(rows[:, :, :, D:ROW].bitcast(I32),
                      pattern=[[P * K, T], [1, K], [0, ROW - D]], base=0, channel_multiplier=K).then_inc(consts, 1)
            pool.wait_ge(consts, N_FILLS)
            pool.affine_select(out=ident[:, :], in_=ident[:, :], compare_op=ALU.not_equal, fill=1.0,
                               base=0, pattern=[[-1, P]], channel_multiplier=1).then_inc(consts, 1)
            pool.affine_select(out=causal[:, :], in_=causal[:, :], compare_op=ALU.is_ge, fill=0.0,
                               base=0, pattern=[[1, P]], channel_multiplier=-1).then_inc(consts, 1)
            pool.affine_select(out=earlier[:, :], in_=earlier[:, :], compare_op=ALU.is_ge, fill=0.0,
                               base=-1, pattern=[[1, P]], channel_multiplier=-1).then_inc(consts, 1)
            hm = headmask[:, :].rearrange("p (h a) -> p h a", h=HEADS)
            pool.affine_select(out=hm, in_=hm, compare_op=ALU.is_ge, fill=0.0,
                               base=0, pattern=[[-DH, HEADS], [0, DH]], channel_multiplier=1).then_inc(consts, 1)
            pool.iota(padding[:, D:ROW].bitcast(I32), pattern=[[0, ROW - D]], base=NOWHERE, channel_multiplier=0).then_inc(consts, 1)
            pool.iota(block_row[:, :], pattern=[[P, BLOCKS]], base=0, channel_multiplier=0,
                      allow_small_or_imprecise_dtypes=True).then_inc(consts, 1)
            pool.memset(one_row[:, :], 1.0).then_inc(consts, 1)
            pool.memset(picked_before_h[:, :], 0.0).then_inc(consts, 1)
            pool.memset(table_f[:, :, :], 0.0).then_inc(consts, 1)
            pool.wait_ge(consts, N_FILLS + 9)
            pool.affine_select(out=hm, in_=hm, compare_op=ALU.is_ge, fill=0.0,
                               base=DH - 1, pattern=[[DH, HEADS], [0, DH]], channel_multiplier=-1).then_inc(consts, 1)

            def norm1(b, t):
                g = T * b + t
                wait(pool, stats_done, g + 1)
                wait(pool, xn_done, g + 1 - T)
                apart(pool)
                pool.tensor_scalar(norm[:, t, 0:1], mv[:, t, 1:2], EPS, None, ALU.add).then_inc(norm_half, 1)
                wait(pool, norm_half, 2 * g + 1)
                pool.tensor_tensor(norm[:, t, 0:1], norm[:, t, 0:1], neghalf[:, :], ALU.pow).then_inc(norm_half, 1)
                wait(pool, norm_half, 2 * g + 2)
                apart(pool)
                pool.tensor_scalar(norm[:, t, 1:2], mv[:, t, 0:1], norm[:, t, 0:1], -1.0, ALU.mult, ALU.mult).then_inc(norm_done, 1)

            def norm2_of(b, t):
                g = T * b + t
                wait(pool, stats2_done, g + 1)
                apart(pool)
                pool.tensor_scalar(norm2_part[:, t, 0:1], mv2[:, t, 1:2], EPS, None, ALU.add).then_inc(norm2_half, 1)
                pool.tensor_scalar(norm2_part[:, t, 1:2], mv2[:, t, 0:1], -1.0, None, ALU.mult).then_inc(norm2_half, 1)
                wait(pool, norm2_half, 3 * g + 2)
                apart(pool)
                pool.tensor_tensor(norm2_at(b, t, 0), norm2_part[:, t, 0:1], neghalf[:, :], ALU.pow).then_inc(norm2_half, 1)
                wait(pool, norm2_half, 3 * g + 3)
                apart(pool)
                pool.tensor_tensor(norm2_at(b, t, 1), norm2_part[:, t, 1:2], norm2_at(b, t, 0), ALU.mult).then_inc(norm2_done, 1)

            def residual(b, t):
                wait(pool, x2_done, T * b + t + 1 - T)
                apart(pool)
                pool.tensor_tensor(xb[:, t, :], tile(x_sb, b, t), bo_bc[:, :], ALU.add).then_inc(xb_done, 1)

            def outer_product(b, t):
                g = T * b + t
                wait(pool, qkv_done, g + 1)
                wait(pool, run_done, g + 1 - T)
                k = qkv[:, t, D:2 * D].rearrange("p (h a) -> p h a", h=HEADS).unsqueeze(3).to_broadcast([P, HEADS, DH, DH])
                v = qkv[:, t, 2 * D:3 * D].rearrange("p (h b) -> p h b", h=HEADS).unsqueeze(2).to_broadcast([P, HEADS, DH, DH])
                pool.tensor_tensor(outer[:, t, :].rearrange("p (h a b) -> p h a b", h=HEADS, a=DH), k, v,
                                   ALU.mult).then_inc(outer_done, 1)

            def take_slots(b, t):
                if t:
                    return
                wait(pool, slot_done, b + 1)
                for u in range(T):
                    wait(pool, dispatch_done[u], 16 * K * b)
                apart(pool)
                pool.tensor_copy(slot[:, :], slot_next[:, :]).then_inc(slots_taken, 1)

            def dispatch(b, t):
                wait(pool, slots_taken, b + 1)
                wait(pool, rows_done, K * (T * b + t + 1))
                wait(pool, dest_moved, T * (b - 1) + t + 1)
                apart(pool)
                for k in range(K):
                    pool.indirect_dma_start(
                        out=dispatched[:, :], out_offset=bass.IndirectOffsetOnAxis(ap=slot[:, t * K + k:t * K + k + 1], axis=0),
                        in_=rows[:, t, k, :], in_offset=None).then_inc(dispatch_done[t], 16)

            def next_destinations(b, t):
                wait(pool, dispatch_done[t], 16 * K * (b + 1))
                apart(pool)
                dest = rows[:, t, :, D:ROW].bitcast(I32)
                pool.tensor_scalar(dest, dest, float(T * P * K), None, ALU.add).then_inc(dest_moved, 1)

            pool.wait_ge(w_att, 6 * 16)
            pool.wait_ge(x_first, 16)
            pool.wait_ge(x_rest, 16 * (B - 1))
            pool.wait_ge(consts, N_CONSTS)
            run_slots(pool, [(0, norm1), (8, norm2_of), (5, residual), (3, outer_product), (17, take_slots),
                             (17, dispatch), (19, next_destinations)], N, T)

            def send_back(i, t):
                wait(pool, y_done, G * i + t + 1)
                apart(pool)
                pool.indirect_dma_start(
                    out=returned[:, :], out_offset=bass.IndirectOffsetOnAxis(ap=xt[:, t, D:D + 1].bitcast(I32), axis=0),
                    in_=y_sb[:, t, :], in_offset=None,
                    bounds_check=K * TOKENS - 1, oob_is_err=False).then_inc(return_done[t], 16)

            with pool.Fori(0, BLOCKS // G) as i:
                for t in range(G):
                    send_back(i, t)

        @block.scalar
        def _(act):
            def normalize(b, t):
                g = T * b + t
                wait(act, norm_done, g + 1)
                wait(act, T1_done, g + 1 - T)
                act.activation(xn[:, t, :], tile(x_sb, b, t), ACT.Identity, bias=norm[:, t, 1:2],
                               scale=norm[:, t, 0:1]).then_inc(xn_done, 1)

            def xnT_out(b, t):
                wait(act, T1_done, T * b + t + 1)
                wait(act, qkv_mm, T * b + t + 1 - T)
                act.activation(xnT[:, t, :], ps_T1, ACT.Identity).then_inc(xnT_done, 1)

            def qT_out(b, t):
                wait(act, qkv_mm, T * b + t + 1)
                wait(act, oT_mm, T * b + t + 1 - T)
                act.activation(qT[:, t, :], ps_qT, ACT.Identity, bias=bq_col[:, 0:1]).then_inc(qT_done, 1)

            def oT_out(b, t):
                wait(act, oT_mm, T * b + t + 1)
                wait(act, att_mm, T * b + t + 1 - T)
                act.activation(oT[:, t, :], ps_oT, ACT.Identity).then_inc(oT_done, 1)

            def normalize2(b, t):
                wait(act, norm2_done, T * b + t + 1)
                wait(act, x2_done, T * b + t + 1)
                wait(act, T2_done, T * b + t + 1 - T)
                act.activation(xn2[:, t, :], tile(x2_sb, b, t), ACT.Identity, bias=norm2_at(b, t, 1),
                               scale=norm2_at(b, t, 0)).then_inc(xn2_done, 1)

            def rows_out(b, t):
                wait(act, dispatch_done[t], 16 * K * b)
                for k in range(K):
                    act.activation(rows[:, t, k, 0:D], tile(x2_sb, b, t), ACT.Identity, bias=norm2_at(b, t, 1),
                                   scale=norm2_at(b, t, 0)).then_inc(rows_done, 1)

            def xn2T_out(b, t):
                wait(act, T2_done, T * b + t + 1)
                wait(act, lg_mm, T * b + t + 1 - T)
                act.activation(xn2T[:, t, :], ps_T2, ACT.Identity).then_inc(xn2T_done, 1)

            def exponentials(b, t):
                if t == T - 1:
                    wait(act, shift_done, b + 1)
                    wait(act, topi_done, T * b)
                    wait(act, gsum_done, b)
                    act.activation(expd[:, :, :], shifted[:, :, :], ACT.Exp).then_inc(exp_done, 1)

            act.wait_ge(x_first, 16)
            act.wait_ge(x_rest, 16 * (B - 1))
            act.wait_ge(w_att, 6 * 16)
            act.wait_ge(consts, N_CONSTS)
            run_slots(act, [(0, normalize), (5, oT_out), (2, qT_out), (1, xnT_out), (10, exponentials), (7, normalize2),
                            (8, xn2T_out), (15, rows_out)], N, T)

            def xT_out(i, t):
                n = G * i + t
                wait(act, TX_done, n + 1)
                wait(act, z_mm, n + 1 - G)
                act.activation(xT[:, t, :], ps_x[t % 2], ACT.Identity).then_inc(xT_done, 1)

            def hT_out(i, t):
                n = G * i + t
                wait(act, TH_done, n + 1)
                wait(act, y_mm, n + 1 - G)
                act.activation(hT[:, t, :, :].rearrange("p c k -> p (c k)"), ps_h[t % 2], ACT.Relu).then_inc(hT_done, 1)

            run_slots(act, [(0, xT_out), (2, hT_out)], BLOCKS, G)

        @block.vector
        def _(dve):
            def stats_of(src, b, t, stats_, mv_, raw, done):
                apart(dve)
                dve.bn_stats(stats_[:, t, :], src).then_inc(raw, 1)
                wait(dve, raw, T * b + t + 1)
                apart(dve)
                dve.bn_aggr(mv_[:, t, :], stats_[:, t, :]).then_inc(done, 1)

            def stats1(b, t):
                wait(dve, norm_done, T * b + t + 1 - T)
                stats_of(tile(x_sb, b, t), b, t, stats, mv, stats_raw, stats_done)

            def qkv_out(b, t):
                g = T * b + t
                wait(dve, qkv_mm, g + 1)
                wait(dve, outer_done, g + 1 - T)
                wait(dve, kv_done, (T - 1) * b)
                dve.tensor_tensor(qkv[:, t, :], ps_qkv, bqkv_bc[:, :], ALU.add).then_inc(qkv_done, 1)

            def state_out(b, t):
                if t == 0:
                    return
                wait(dve, kv_done, (T - 1) * b + t)
                wait(dve, att_mm, T * b + t - 2)
                wait(dve, oT_mm, T * b + t + 1 - T)
                dve.tensor_tensor(state[:, t, :], ps_state, headmask[:, :], ALU.mult).then_inc(state_done, 1)

            def attend(b, t):
                g = T * b + t
                wait(dve, run_done, g + 1)
                wait(dve, o_done, g - 1)
                q = qkv[:, t, 0:D].rearrange("p (h a) -> p h a", h=HEADS).unsqueeze(3).to_broadcast([P, HEADS, DH, DH])
                run = ps_run[t % 2].rearrange("p u f -> p (u f)").rearrange("p (h a b) -> p h a b", h=HEADS, a=DH)
                dve.tensor_tensor(prod[:, t % 2, :].rearrange("p (h a b) -> p h a b", h=HEADS, a=DH), run, q,
                                  ALU.mult).then_inc(prod_done, 1)
                wait(dve, prod_done, g + 1)
                wait(dve, oT_mm, g + 1 - T)
                dve.tensor_reduce(o_sb[:, t, :].rearrange("p (h b) -> p h b", h=HEADS),
                                  prod[:, t % 2, :].rearrange("p (h a b) -> p h b a", h=HEADS, a=DH),
                                  AX_X, ALU.add).then_inc(o_done, 1)

            def add_residual(b, t):
                g = T * b + t
                wait(dve, att_mm, g + 1)
                wait(dve, xb_done, g + 1)
                dve.tensor_tensor(tile(x2_sb, b, t), ps_att, xb[:, t, :], ALU.add).then_inc(x2_done, 1)
                wait(dve, x2_done, g + 1)
                wait(dve, norm2_done, g + 1 - T)
                stats_of(tile(x2_sb, b, t), b, t, stats2, mv2, stats2_raw, stats2_done)

            def over_e(ap):
                return ap[:, :].unsqueeze(2).to_broadcast([P, T, E])

            def softmax_start(b, t):
                if t < T - 1:
                    return
                wait(dve, lg_mm, T * (b + 1))
                wait(dve, att_mm, T * b + t + 4, N)
                dve.tensor_reduce(gmax[:, :], ps_lg, AX_X, ALU.max).then_inc(gmax_done, 1)
                wait(dve, gmax_done, b + 1)
                dve.tensor_tensor(shifted[:, :, :], ps_lg, over_e(gmax), ALU.subtract).then_inc(shift_done, 1)

            def softmax_end(b, t):
                if t < T - 1:
                    return
                wait(dve, exp_done, b + 1)
                dve.tensor_reduce(gsum[:, :], expd[:, :, :], AX_X, ALU.add).then_inc(gsum_done, 1)
                for u in range(T):
                    dve.max(top[:, u, :], expd[:, u, :]).then_inc(top_done, 1)
                wait(dve, gsum_done, b + 1)
                dve.reciprocal(grec[:, :], gsum[:, :]).then_inc(grec_done, 1)
                for u in range(T):
                    wait(dve, top_done, T * b + u + 1)
                    apart(dve)
                    dve.max_index(top_i[:, u, :], top[:, u, :], expd[:, u, :]).then_inc(topi_done, 1)
                wait(dve, grec_done, b + 1)
                dve.tensor_tensor(chosen[:, bass.ds(T * b * K, T * K)].rearrange("p (t k) -> p t k", t=T), top[:, :, 0:K],
                                  grec[:, :].unsqueeze(2).to_broadcast([P, T, K]), ALU.mult).then_inc(chosen_done, 1)
                wait(dve, topi_done, T * (b + 1))
                dve.tensor_copy(top_f[:, :, :], top_i[:, :, 0:K]).then_inc(topf_done, 1)

            def count(b, t):
                if t < T - 1:
                    return
                wait(dve, topf_done, b + 1)
                dve.tensor_tensor(pick[:, :, :, :], top_f[:, :, :].unsqueeze(3).to_broadcast([P, T, K, E]),
                                  expert_no[:, :].unsqueeze(1).unsqueeze(1).to_broadcast([P, T, K, E]),
                                  ALU.is_equal).then_inc(pick_done, 1)
                wait(dve, pick_done, b + 1)
                wait(dve, place_mm, b)
                dve.tensor_tensor(picked[:, :, :], pick[:, :, 0, :], pick[:, :, 1, :], ALU.add).then_inc(picked_done, 1)

            def places(b, t):
                if t < T - 1:
                    return
                wait(dve, place_mm, b + 1)
                wait(dve, lg_mm, T * b + t + 3, N)
                wait(dve, att_mm, T * b + t + 6, N)
                dve.tensor_tensor(place[:, :, :], ps_place, region_of[:, :].unsqueeze(1).to_broadcast([P, T, E]),
                                  ALU.add).then_inc(place_done, 1)
                dve.tensor_reduce(picked_sum[:, :], picked[:, :, :].rearrange("p t e -> p e t"), AX_X, ALU.add).then_inc(psum_done, 1)
                wait(dve, place_done, b + 1)
                dve.tensor_tensor(place_of[:, :, :, :], pick[:, :, :, :], place[:, :, :].unsqueeze(2).to_broadcast([P, T, K, E]),
                                  ALU.mult).then_inc(placeof_done, 1)
                wait(dve, psum_done, b + 1)
                dve.tensor_tensor(picked_before[:, :], picked_before[:, :], picked_sum[:, :], ALU.add).then_inc(before_done, 1)
                wait(dve, placeof_done, b + 1)
                dve.tensor_reduce(slot_f[:, :, :], place_of[:, :, :, :], AX_X, ALU.add).then_inc(slotf_done, 1)
                wait(dve, before_done, b + 1)
                dve.tensor_copy(picked_before_h[:, :], picked_before[:, :]).then_inc(before_h_done, 1)
                wait(dve, slotf_done, b + 1)
                wait(dve, slots_taken, b)
                dve.tensor_copy(slot_next[:, :].rearrange("p (t k) -> p t k", t=T), slot_f[:, :, :]).then_inc(slot_done, 1)

            dve.wait_ge(x_first, 16)
            dve.wait_ge(x_rest, 16 * (B - 1))
            dve.wait_ge(w_att, 6 * 16)
            dve.wait_ge(consts, N_CONSTS)
            run_slots(dve, [(0, stats1), (11, softmax_start), (13, places), (5, state_out), (8, add_residual), (3, qkv_out),
                            (11, softmax_end), (4, attend), (11, count)], N, T)

            steps = 0

            def step(ins):
                nonlocal steps
                steps += 1
                ins.then_inc(table_step, 1)
                dve.wait_ge(table_step, steps)

            dve.wait_ge(cnt_mm, 1)
            step(dve.tensor_copy(cnt[:, :], ps_cnt))
            step(dve.tensor_tensor(end_row_f[:, :], cnt[:, :], region_of[0:1, :], ALU.add))
            dve.tensor_copy(end_row[:, :], end_row_f[:, :]).then_inc(end_row_done, 1)
            step(dve.tensor_scalar(cnt[:, :], cnt[:, :], float(P - 1), None, ALU.add))
            step(dve.tensor_copy(cnt_i[:, :], cnt[:, :]))
            step(dve.tensor_scalar(cnt_i[:, :], cnt_i[:, :], P.bit_length() - 1, None, ALU.arith_shift_right))
            step(dve.tensor_copy(n_blocks[:, :], cnt_i[:, :]))
            step(dve.tensor_tensor_scan(end_block[:, :], one_row[:, :], n_blocks[:, :], 0.0, ALU.mult, ALU.add))
            step(dve.tensor_scalar(jump[:, :], n_blocks[:, :], -float(P), float(REGION), ALU.mult, ALU.add))
            step(dve.tensor_tensor(past[:, :, :], block_no[:, :].unsqueeze(2).to_broadcast([1, BLOCKS, E]),
                                   end_block[:, :].unsqueeze(1).to_broadcast([1, BLOCKS, E]), ALU.is_ge))
            step(dve.tensor_tensor(skipped[:, :, :], past[:, :, :], jump[:, :].unsqueeze(1).to_broadcast([1, BLOCKS, E]), ALU.mult))
            step(dve.tensor_reduce(blk[:, :, 0], skipped[:, :, :], AX_X, ALU.add))
            step(dve.tensor_reduce(blk[:, :, 1], past[:, :, :], AX_X, ALU.add))
            step(dve.tensor_tensor(blk[:, :, 0], blk[:, :, 0], block_row[:, :], ALU.add))
            step(dve.tensor_scalar(table_f[:, :, 0], blk[:, :, 0], float(PAD_BLOCK), None, ALU.min))
            step(dve.tensor_scalar(table_f[:, :, 1], blk[:, :, 1], float(E - 1), float(H), ALU.min, ALU.mult))
            step(dve.tensor_scalar(table_f[:, :, 2], blk[:, :, 1], float(E - 1), float(D), ALU.min, ALU.mult))
            dve.tensor_copy(table[:, :], table_f[:, :, :].rearrange("o n w -> o (n w)")).then_inc(table_done, 1)

            dve.wait_ge(table_done, 1)
            dve.wait_ge(w_ffn, (3 + HC) * 16)

            def z_out(i, t):
                n = G * i + t
                wait(dve, z_mm, n + 1)
                wait(dve, TH_done, n + 1 - G)
                at = dve.value_load(table[0:1, bass.ds(n * 4 + 1, 1)], min_val=0, max_val=(E - 1) * H)
                dve.tensor_tensor(z_sb[:, t, :], ps_z[t % 2], b1_bc[:, bass.ds(at, H)], ALU.add).then_inc(z_done, 1)

            def y_out(i, t):
                n = G * i + t
                wait(dve, y_mm, n + 1)
                wait(dve, return_done[t], 16 * i)
                at = dve.value_load(table[0:1, bass.ds(n * 4 + 2, 1)], min_val=0, max_val=(E - 1) * D)
                dve.tensor_tensor(y_sb[:, t, :], ps_y[t % 2], b2_bc[:, bass.ds(at, D)], ALU.add).then_inc(y_done, 1)

            run_slots(dve, [(1, z_out), (3, y_out)], BLOCKS, G)

            for b in range(B):
                dve.wait_ge(back_in[b], 16)
                for k in range(K):
                    for t in range(T):
                        g = T * b + t
                        if k:
                            dve.wait_ge(first_added, g + 1)
                        dst = x2_sb[:, g * D:(g + 1) * D]
                        dve.scalar_tensor_tensor(out=dst, in0=back[:, (g * K + k) * D:(g * K + k + 1) * D],
                                                 scalar=chosen[:, g * K + k:g * K + k + 1], in1=dst,
                                                 op0=ALU.mult, op1=ALU.add).then_inc(both_added if k else first_added, 1)

        @block.tensor
        def _(pe):
            def transpose1(b, t):
                g = T * b + t
                wait(pe, xn_done, g + 1)
                wait(pe, oT_done, g - 3)
                pe.transpose(ps_T1, xn[:, t, :], ident[:, :]).then_inc(T1_done, 1)

            def project(b, t):
                g = T * b + t
                wait(pe, xnT_done, g + 1)
                wait(pe, xn2T_done, g - 6)
                wait(pe, qkv_done, g)
                pe.matmul(ps_qT, wqkv_sb[:, 0:D], xnT[:, t, :], start=True, stop=True)
                pe.matmul(ps_qkv, xnT[:, t, :], wqkv_sb[:, :], start=True, stop=True).then_inc(qkv_mm, 1)

            def running_sums(b, t):
                g = T * b + t
                wait(pe, outer_done, g + 1)
                wait(pe, prod_done, g - 1)
                for u in range(2):
                    mm = pe.matmul(ps_run[t % 2][:, u, :], causal[:, :], outer[:, t, 512 * u:512 * (u + 1)],
                                   start=True, stop=True)
                mm.then_inc(run_done, 1)

            def sum_state(b, t):
                if t == 0:
                    return
                wait(pe, qkv_done, T * b + t)
                wait(pe, state_done, (T - 1) * b + t - 1)
                wait(pe, x2_done, T * b + t - 3)
                for u in range(t):
                    mm = pe.matmul(ps_state, qkv[:, u, D:2 * D], qkv[:, u, 2 * D:3 * D], start=(u == 0), stop=(u == t - 1))
                mm.then_inc(kv_done, 1)

            def o_transposed(b, t):
                g = T * b + t
                wait(pe, o_done, g + 1)
                wait(pe, xnT_done, g + 4, N)
                wait(pe, oT_done, g)
                mm = pe.matmul(ps_oT, o_sb[:, t, :], ident[:, :], start=True, stop=(t == 0))
                if t:
                    wait(pe, state_done, (T - 1) * b + t)
                    wait(pe, qT_done, g + 1)
                    mm = pe.matmul(ps_oT, state[:, t, :], qT[:, t, :], start=False, stop=True)
                mm.then_inc(oT_mm, 1)

            def project_out(b, t):
                g = T * b + t
                wait(pe, oT_done, g + 1)
                wait(pe, x2_done, g)
                wait(pe, state_done, (T - 1) * b + min(t + 2, T - 1) + (t == T - 1), (T - 1) * B)
                pe.matmul(ps_att, oT[:, t, :], wo_sb[:, :], start=True, stop=True).then_inc(att_mm, 1)

            def transpose2(b, t):
                g = T * b + t
                wait(pe, xn2_done, g + 1)
                wait(pe, qT_done, g + 7, N)
                wait(pe, xn2T_done, g)
                pe.transpose(ps_T2, xn2[:, t, :], ident[:, :]).then_inc(T2_done, 1)

            def gate(b, t):
                wait(pe, xn2T_done, T * b + t + 1)
                wait(pe, x2_done, T * b + t + 3, N)
                if t == 0:
                    wait(pe, shift_done, b)
                if t == 2:
                    wait(pe, place_done, b)
                pe.matmul(ps_lg[:, t, :], xn2T[:, t, :], wg_sb[:, :], start=True, stop=True).then_inc(lg_mm, 1)

            def rank(b, t):
                if t < T - 1:
                    return
                wait(pe, picked_done, b + 1)
                wait(pe, x2_done, T * b + t + 5, N)
                wait(pe, before_h_done, b)
                pe.matmul(ps_place, earlier[:, :], picked[:, :, :], start=True, stop=False, skip_group_check=True)
                for u in range(T - 1):
                    pe.matmul(ps_place[:, u + 1:T, :], ones[:, :],
                              picked[:, u, :].unsqueeze(1).to_broadcast([P, T - 1 - u, E]),
                              start=False, stop=False, skip_group_check=True)
                mm = pe.matmul(ps_place, ones[:, :], picked_before_h[:, :].unsqueeze(1).to_broadcast([P, T, E]),
                               start=False, stop=True, skip_group_check=True)
                mm.then_inc(place_mm, 1)

            pe.wait_ge(consts, N_CONSTS)
            pe.wait_ge(w_att, 6 * 16)
            run_slots(pe, [(4, o_transposed), (1, project), (0, transpose1), (2, sum_state), (8, gate), (10, rank),
                           (5, project_out), (2, running_sums), (7, transpose2)], N, T)

            pe.wait_ge(before_h_done, B)
            pe.matmul(ps_cnt, ones[:, 0:1], picked_before_h[:, :], start=True, stop=True).then_inc(cnt_mm, 1)

            pe.wait_ge(table_done, 1)
            pe.wait_ge(w_ffn, (3 + HC) * 16)

            def transpose_x(i, t):
                n = G * i + t
                pe.wait_ge(xt_in[t], 16 * (i + 1))
                wait(pe, xT_done, n - 1)
                pe.transpose(ps_x[t % 2], xt[:, t, 0:D], ident[:, :]).then_inc(TX_done, 1)

            def hidden(i, t):
                n = G * i + t
                wait(pe, xT_done, n + 1)
                wait(pe, z_done, n - 1)
                at = pe.value_load(table[0:1, bass.ds(n * 4 + 1, 1)], min_val=0, max_val=(E - 1) * H)
                pe.matmul(ps_z[t % 2], xT[:, t, :], w1_sb[:, bass.ds(at, H)], start=True, stop=True).then_inc(z_mm, 1)

            def transpose_h(i, t):
                n = G * i + t
                wait(pe, z_done, n + 1)
                wait(pe, hT_done, n - 1)
                for c in range(HC):
                    mm = pe.transpose(ps_h[t % 2][:, c * P:(c + 1) * P], z_sb[:, t, c * P:(c + 1) * P], ident[:, :])
                mm.then_inc(TH_done, 1)

            def output(i, t):
                n = G * i + t
                wait(pe, hT_done, n + 1)
                wait(pe, y_done, n - 1)
                at = pe.value_load(table[0:1, bass.ds(n * 4 + 2, 1)], min_val=0, max_val=(E - 1) * D)
                for c in range(HC):
                    mm = pe.matmul(ps_y[t % 2], hT[:, t, c, :], w2_sb[:, c, bass.ds(at, D)], start=(c == 0), stop=(c == HC - 1))
                mm.then_inc(y_mm, 1)

            run_slots(pe, [(0, transpose_x), (1, hidden), (2, transpose_h), (3, output)], BLOCKS, G)


_OUT = (8, 512, 128)


def kernel(L0_attn_x, L0_attn_wq_w, L0_attn_wq_b, L0_attn_wk_w, L0_attn_wk_b, L0_attn_wv_w, L0_attn_wv_b,
           L0_attn_wo_w, L0_attn_wo_b, L0_ffn_Wg, L0_ffn_W1, L0_ffn_b1, L0_ffn_W2, L0_ffn_b2):
    import numpy as np
    import concourse.bacc as bacc
    from concourse.bass_utils import run_bass_kernel_spmd

    arrays = {
        "x": L0_attn_x,
        "w_qkv": np.concatenate([np.asarray(w).T for w in (L0_attn_wq_w, L0_attn_wk_w, L0_attn_wv_w)], axis=1),
        "b_qkv": np.concatenate([np.asarray(b) for b in (L0_attn_wq_b, L0_attn_wk_b, L0_attn_wv_b)]),
        "b_q": np.asarray(L0_attn_wq_b).reshape(-1, 1),
        "w_o": np.asarray(L0_attn_wo_w).T,
        "b_o": L0_attn_wo_b,
        "w_gate": L0_ffn_Wg,
        "w1": L0_ffn_W1,
        "b1": np.asarray(L0_ffn_b1).reshape(-1),
        "w2": L0_ffn_W2,
        "b2": np.asarray(L0_ffn_b2).reshape(-1),
    }
    arrays = {name: np.ascontiguousarray(a) for name, a in arrays.items()}
    nc = bacc.Bacc("TRN2", target_bir_lowering=False, num_devices=1)
    args = {name: nc.dram_tensor(name, a.shape, mybir.dt.from_np(a.dtype), kind="ExternalInput").ap()
            for name, a in arrays.items()}
    out = nc.dram_tensor("out", _OUT, F32, kind="ExternalOutput").ap()
    preln_linear_attention_moe(nc, out=out, **args)
    result = run_bass_kernel_spmd(nc, [arrays], core_ids=[0])
    return result.results[0]["out"]
```

```python
from contextlib import ExitStack

import concourse.bass as bass
from concourse import mybir

ALU = mybir.AluOpType
ACT = mybir.ActivationFunctionType
AX_X = mybir.AxisListType.X
F32 = mybir.dt.float32
BF16 = mybir.dt.bfloat16
I32 = mybir.dt.int32
U32 = mybir.dt.uint32

P = 128
HEADS = 16
DH = P // HEADS
EPS = 1e-5


def wait(eng, sem, value, most=None):
    if isinstance(value, int):
        value = value if most is None else min(value, most)
        if value <= 0:
            return
    eng.wait_ge(sem, value)


def run_slots(eng, stages, n_tiles, group, at_group=None):
    deepest = max(lag for lag, _ in stages)
    first = -(-deepest // group) * group + group
    for s in range(first):
        if at_group and s % group == 0:
            at_group(s // group)
        for lag, stage in stages:
            if s >= lag:
                stage((s - lag) // group, (s - lag) % group)
    with eng.Fori(first // group, n_tiles // group) as i:
        if at_group:
            at_group(i)
        for t in range(group):
            for lag, stage in stages:
                stage(i + (t - lag) // group, (t - lag) % group)
    for s in range(n_tiles, n_tiles + deepest):
        if at_group and s % group == 0:
            at_group(s // group)
        for lag, stage in stages:
            if s - lag < n_tiles:
                stage((s - lag) // group, (s - lag) % group)


def preln_linear_attention_moe(nc, x, w_qkv, b_qkv, b_q, w_o, b_o, w_gate, w1, b1, w2, b2, out):
    B, L, D = x.shape
    E, _, H = w1.shape
    T = L // P
    N = B * T
    TOKENS = N * P
    HC = H // P
    OUTER = D * DH
    K = 2
    ROW = D + 4
    REGION = TOKENS + P
    PAD_BLOCK = E * REGION
    NOWHERE = K * TOKENS
    G = 8
    HIDDEN, OUTPUT = 1, 3
    BLOCKS = -(-((K * TOKENS + E * (P - 1)) // P) // G) * G
    assert D == P and T == 4 and H == HC * P

    with ExitStack() as ctx:
        def sb(name, shape, dt=F32):
            return ctx.enter_context(nc.sbuf_tensor(name, shape, dt))

        def sem(name):
            return ctx.enter_context(nc.semaphore(name))

        dispatched = nc.dram_tensor("dispatched", [PAD_BLOCK + P, ROW], F32, kind="Internal").ap()
        returned = nc.dram_tensor("returned", [K * TOKENS, D], F32, kind="Internal").ap()

        ident = sb("ident", [P, P])
        causal = sb("causal", [P, P])
        earlier = sb("earlier", [P, P], BF16)
        ones = sb("ones", [P, P], BF16)
        headmask = sb("headmask", [P, P])
        eps = sb("eps", [P, 1])
        dest_in = sb("dest_in", [P, T, K])
        dest_from = sb("dest_from", [P, B])
        expert_no = sb("expert_no", [P, E])
        region_of = sb("region_of", [P, E])
        block_no = sb("block_no", [1, BLOCKS])
        block_row = sb("block_row", [1, BLOCKS])
        padding = sb("padding", [P, ROW])
        wqkv_sb = sb("wqkv_sb", [P, 3 * D])
        bqkv_bc = sb("bqkv_bc", [P, 3 * D])
        bq_col = sb("bq_col", [P, 1])
        wo_sb = sb("wo_sb", [P, D])
        bo_bc = sb("bo_bc", [P, D])
        wg_sb = sb("wg_sb", [P, E])
        w1_sb = sb("w1_sb", [P, E * H])
        b1_bc = sb("b1_bc", [P, E * H])
        w2_sb = sb("w2_sb", [P, HC, E * D])
        b2_bc = sb("b2_bc", [P, E * D])
        x_sb = sb("x_sb", [P, N * D])
        x2_sb = sb("x2_sb", [P, N * D])
        stats = sb("stats", [P, N, 6])
        mv = sb("mv", [P, N, 2])
        std = sb("std", [P, N])
        norm = sb("norm", [P, N * 2])
        back = sb("back", [P, N * K * D])
        chosen = sb("chosen", [P, N * K])
        xn = sb("xn", [P, T, D])
        xnT = sb("xnT", [P, T, P])
        qT = sb("qT", [P, T, P])
        qkv = sb("qkv", [P, T, 3 * D])
        outer = sb("outer", [P, T, OUTER])
        state = sb("state", [P, T, D])
        prod = sb("prod", [P, 2, OUTER])
        o_sb = sb("o_sb", [P, T, D])
        oT = sb("oT", [P, T, P])
        stats2 = sb("stats2", [P, T, 6])
        mv2 = sb("mv2", [P, T, 2])
        std2 = sb("std2", [P, T])
        norm2 = sb("norm2", [P, N * 2])
        xn2 = sb("xn2", [P, T, D])
        rows = sb("rows", [P, T, K, ROW])
        xn2T = sb("xn2T", [P, T, P])
        gmax = sb("gmax", [P, T])
        shifted = sb("shifted", [P, T, E])
        expd = sb("expd", [P, T, E])
        gsum = sb("gsum", [P, T])
        grec = sb("grec", [P, T])
        top = sb("top", [P, T, E])
        top_i = sb("top_i", [P, T, E], U32)
        top_f = sb("top_f", [P, T, K])
        pick = sb("pick", [P, T, K, E])
        picked = sb("picked", [P, T, E], BF16)
        picked_sum = sb("picked_sum", [P, E])
        picked_before = sb("picked_before", [P, E])
        picked_before_h = sb("picked_before_h", [P, E], BF16)
        place = sb("place", [P, T, E])
        place_of = sb("place_of", [P, T, K, E])
        slot_f = sb("slot_f", [P, T, K])
        slot_next = sb("slot_next", [P, T * K], I32)
        slot = sb("slot", [P, T * K], I32)
        cnt_i = sb("cnt_i", [1, E], I32)
        end_row = sb("end_row", [1, E], I32)
        n_blocks = sb("n_blocks", [1, E])
        one_row = sb("one_row", [1, E])
        end_block = sb("end_block", [1, E])
        jump = sb("jump", [1, E])
        past = sb("past", [1, BLOCKS, E])
        skipped = sb("skipped", [1, BLOCKS, E])
        row_f = sb("row_f", [1, BLOCKS])
        expert_f = sb("expert_f", [1, BLOCKS])
        row_at = sb("row_at", [1, BLOCKS], I32)
        w1_at = sb("w1_at", [1, BLOCKS + G], I32)
        w2_at = sb("w2_at", [1, BLOCKS + G], I32)
        xt = sb("xt", [P, G, ROW])
        xT = sb("xT", [P, G, P])
        z_sb = sb("z_sb", [P, G, H])
        hT = sb("hT", [P, G, HC, P])
        y_sb = sb("y_sb", [P, G, D])

        ps = ctx.enter_context(nc.psum_tensor("ps", [P, 8, 512], F32))
        ps_T1 = ps[:, 0, 0:P]
        ps_oT = ps[:, 0, P:2 * P]
        ps_qT = ps[:, 1, 0:P]
        ps_T2 = ps[:, 1, P:2 * P]
        ps_run = [ps[:, 2:4, :], ps[:, 4:6, :]]
        ps_qkv = ps[:, 6, 0:3 * D]
        ps_state = ps[:, 7, 0:D]
        ps_att = ps[:, 7, P:2 * P]
        ps_lg = ps[:, 7, 2 * P:2 * P + T * E].rearrange("p (t e) -> p t e", t=T)
        ps_place = ps[:, 7, 3 * P:3 * P + T * E].rearrange("p (t e) -> p t e", t=T)
        ps_cnt = ps[0:1, 7, 3 * P + T * E:3 * P + T * E + E]
        ps_x = [ps[:, u, 0:P] for u in range(2)]
        ps_z = [ps[:, 2 + u, 0:H] for u in range(2)]
        ps_h = [ps[:, 4 + u, 0:H] for u in range(2)]
        ps_y = [ps[:, 6 + u, 0:D] for u in range(2)]

        consts, passed = sem("consts"), sem("passed")
        x_in = [sem(f"x_in{b}") for b in range(B)]
        w_att, w_ffn = sem("w_att"), sem("w_ffn")
        stats_raw, stats_done, std_done, rstd_done, norm_done = sem("stats_raw"), sem("stats_done"), sem("std_done"), sem("rstd_done"), sem("norm_done")
        xn_done, T1_done, xnT_done = sem("xn_done"), sem("T1_done"), sem("xnT_done")
        qkv_mm, qT_done, qkv_done = sem("qkv_mm"), sem("qT_done"), sem("qkv_done")
        outer_done, run_done, kv_done, state_done = sem("outer_done"), sem("run_done"), sem("kv_done"), sem("state_done")
        prod_done, o_done, oT_mm, oT_done = sem("prod_done"), sem("o_done"), sem("oT_mm"), sem("oT_done")
        att_mm, xb_done, x2_done = sem("att_mm"), sem("xb_done"), sem("x2_done")
        stats2_raw, stats2_done, std2_done, rstd2_done, norm2_done = (
            sem("stats2_raw"), sem("stats2_done"), sem("std2_done"), sem("rstd2_done"), sem("norm2_done"))
        xn2_done, rows_done, T2_done, xn2T_done = sem("xn2_done"), sem("rows_done"), sem("T2_done"), sem("xn2T_done")
        lg_mm = sem("lg_mm")
        gmax_done, shift_done, exp_done, gsum_done = sem("gmax_done"), sem("shift_done"), sem("exp_done"), sem("gsum_done")
        grec_done, top_done, topi_done, topf_done = sem("grec_done"), sem("top_done"), sem("topi_done"), sem("topf_done")
        chosen_done, pick_done, picked_done, place_mm = sem("chosen_done"), sem("pick_done"), sem("picked_done"), sem("place_mm")
        psum_done, before_done, before_h_done = sem("psum_done"), sem("before_done"), sem("before_h_done")
        place_done, placeof_done, slotf_done, slot_done = sem("place_done"), sem("placeof_done"), sem("slotf_done"), sem("slot_done")
        slots_taken = sem("slots_taken")
        dispatch_done = [sem(f"dispatch_done{t}") for t in range(T)]
        cnt_mm, table_step, end_row_done, table_done, pads_done = sem("cnt_mm"), sem("table_step"), sem("end_row_done"), sem("table_done"), sem("pads_done")
        xt_in = [sem(f"xt_in{t}") for t in range(G)]
        TX_done, xT_done, z_mm, z_done, TH_done, hT_done, y_mm, y_done = (
            sem("TX_done"), sem("xT_done"), sem("z_mm"), sem("z_done"), sem("TH_done"), sem("hT_done"), sem("y_mm"), sem("y_done"))
        dest_done = sem("dest_done")
        return_done = [sem(f"return_done{t}") for t in range(G)]
        back_in = [sem(f"back_in{b}") for b in range(B)]
        first_added, both_added = sem("first_added"), sem("both_added")
        stored = sem("stored")

        def tile(buf, b, t):
            return buf[:, bass.ds((T * b + t) * P, P)]

        def norm_at(buf, b, t, w):
            return buf[:, bass.ds((T * b + t) * 2 + w, 1)]

        def bcast(ap):
            return ap.partition_broadcast(P)

        x_t = x.rearrange("b (t p) d -> b p t d", p=P)
        out_t = out.rearrange("b (t p) d -> b p t d", p=P)
        back_t = returned.rearrange("(b t p k) d -> b p t (k d)", b=B, t=T, k=K)

        N_FILLS = 14
        N_CONSTS = N_FILLS + 11
        block = ctx.enter_context(nc.Block())

        def apart(eng):
            eng.sem_inc(passed, 1)

        def read(engine, numbers, most):
            return nc.values_load_multi_w_load_instructions(
                numbers, engines=[engine], min_val=0, max_val=most,
                skip_runtime_bounds_check_because="the table's steps bound them")[1]

        @block.sync
        def _(sp):
            def load_x(b):
                return sp.dma_start(x_sb[:, b * T * D:(b + 1) * T * D].rearrange("p (t d) -> p t d", t=T), x_t[b])
            for b in range(B):
                load_x(b).then_inc(x_in[b], 16)
            sp.dma_start(wqkv_sb[:, :], w_qkv).then_inc(w_att, 16)
            sp.dma_start(bqkv_bc[:, :], bcast(b_qkv)).then_inc(w_att, 16)
            sp.dma_start(bq_col[:, :], b_q).then_inc(w_att, 16)
            sp.dma_start(wo_sb[:, :], w_o).then_inc(w_att, 16)
            sp.dma_start(bo_bc[:, :], bcast(b_o)).then_inc(w_att, 16)
            sp.dma_start(wg_sb[:, :], w_gate).then_inc(w_att, 16)
            sp.dma_start(w1_sb[:, :].rearrange("d (e h) -> d e h", e=E), w1.rearrange("e d h -> d e h")).then_inc(w_ffn, 16)
            sp.dma_start(b1_bc[:, :], bcast(b1)).then_inc(w_ffn, 16)
            for c in range(HC):
                sp.dma_start(w2_sb[:, c, :].rearrange("p (e d) -> p e d", e=E),
                             w2[:, c * P:(c + 1) * P, :].rearrange("e p d -> p e d")).then_inc(w_ffn, 16)
            sp.dma_start(b2_bc[:, :], bcast(b2)).then_inc(w_ffn, 16)
            sp.wait_ge(consts, N_CONSTS)
            sp.dma_start(dispatched[PAD_BLOCK:PAD_BLOCK + P, :], padding[:, :]).then_inc(pads_done, 16)

            sp.wait_ge(end_row_done, 1)
            for row in read(mybir.EngineType.SP, end_row[0:1, 0:E], PAD_BLOCK):
                sp.dma_start(dispatched[bass.ds(row, P), :], padding[:, :]).then_inc(pads_done, 16)
            sp.wait_ge(table_done, 3)
            sp.wait_ge(pads_done, 16 * (E + 1))
            for t in range(T):
                sp.wait_ge(dispatch_done[t], 16 * B * K)

            def load_block(i, t, row):
                wait(sp, TX_done, G * (i - 1) + t + 1)
                apart(sp)
                wait(sp, return_done[t], 16 * i)
                apart(sp)
                sp.dma_start(xt[:, t, :], dispatched[bass.ds(row, P), :]).then_inc(xt_in[t], 16)

            rows_at = read(mybir.EngineType.SP, row_at[0:1, 0:G], PAD_BLOCK)
            for t in range(G):
                load_block(0, t, rows_at[t])
            with sp.Fori(1, BLOCKS // G) as i:
                rows_at = read(mybir.EngineType.SP, row_at[0:1, bass.ds(G * i, G)], PAD_BLOCK)
                for t in range(G):
                    load_block(i, t, rows_at[t])

            for t in range(G):
                sp.wait_ge(return_done[t], 16 * (BLOCKS // G))
            for b in range(B):
                sp.dma_start(back[:, b * T * K * D:(b + 1) * T * K * D].rearrange("p (t f) -> p t f", t=T),
                             back_t[b]).then_inc(back_in[b], 16)
            for b in range(B):
                sp.wait_ge(both_added, (b + 1) * T)
                sp.dma_start(out_t[b], x2_sb[:, b * T * D:(b + 1) * T * D].rearrange("p (t d) -> p t d", t=T)).then_inc(stored, 16)
            sp.wait_ge(stored, 16 * B)

        @block.gpsimd
        def _(pool):
            pool.memset(ident[:, :], 0.0).then_inc(consts, 1)
            pool.memset(causal[:, :], 1.0).then_inc(consts, 1)
            pool.memset(earlier[:, :], 1.0).then_inc(consts, 1)
            pool.memset(ones[:, :], 1.0).then_inc(consts, 1)
            pool.memset(headmask[:, :], 1.0).then_inc(consts, 1)
            pool.memset(eps[:, :], EPS).then_inc(consts, 1)
            pool.memset(padding[:, :], 0.0).then_inc(consts, 1)
            pool.memset(picked_before[:, :], 0.0).then_inc(consts, 1)
            pool.iota(expert_no[:, :], pattern=[[1, E]], base=0, channel_multiplier=0,
                      allow_small_or_imprecise_dtypes=True).then_inc(consts, 1)
            pool.iota(region_of[:, :], pattern=[[REGION, E]], base=0, channel_multiplier=0,
                      allow_small_or_imprecise_dtypes=True).then_inc(consts, 1)
            pool.iota(block_no[:, :], pattern=[[1, BLOCKS]], base=0, channel_multiplier=0,
                      allow_small_or_imprecise_dtypes=True).then_inc(consts, 1)
            pool.iota(dest_in[:, :, :], pattern=[[P * K, T], [1, K]], base=0, channel_multiplier=K,
                      allow_small_or_imprecise_dtypes=True).then_inc(consts, 1)
            pool.iota(dest_from[:, :], pattern=[[T * P * K, B]], base=0, channel_multiplier=0,
                      allow_small_or_imprecise_dtypes=True).then_inc(consts, 1)
            pool.memset(rows[:, :, :, :], 0.0).then_inc(consts, 1)
            pool.wait_ge(consts, N_FILLS)
            pool.affine_select(out=ident[:, :], in_=ident[:, :], compare_op=ALU.not_equal, fill=1.0,
                               base=0, pattern=[[-1, P]], channel_multiplier=1).then_inc(consts, 1)
            pool.affine_select(out=causal[:, :], in_=causal[:, :], compare_op=ALU.is_ge, fill=0.0,
                               base=0, pattern=[[1, P]], channel_multiplier=-1).then_inc(consts, 1)
            pool.affine_select(out=earlier[:, :], in_=earlier[:, :], compare_op=ALU.is_ge, fill=0.0,
                               base=-1, pattern=[[1, P]], channel_multiplier=-1).then_inc(consts, 1)
            hm = headmask[:, :].rearrange("p (h a) -> p h a", h=HEADS)
            pool.affine_select(out=hm, in_=hm, compare_op=ALU.is_ge, fill=0.0,
                               base=0, pattern=[[-DH, HEADS], [0, DH]], channel_multiplier=1).then_inc(consts, 1)
            pool.iota(padding[:, D:ROW].bitcast(I32), pattern=[[0, ROW - D]], base=NOWHERE, channel_multiplier=0).then_inc(consts, 1)
            pool.iota(block_row[:, :], pattern=[[P, BLOCKS]], base=0, channel_multiplier=0,
                      allow_small_or_imprecise_dtypes=True).then_inc(consts, 1)
            pool.memset(one_row[:, :], 1.0).then_inc(consts, 1)
            pool.memset(picked_before_h[:, :], 0.0).then_inc(consts, 1)
            pool.memset(w1_at[:, :], 0).then_inc(consts, 1)
            pool.memset(w2_at[:, :], 0).then_inc(consts, 1)
            pool.wait_ge(consts, N_FILLS + 10)
            pool.affine_select(out=hm, in_=hm, compare_op=ALU.is_ge, fill=0.0,
                               base=DH - 1, pattern=[[DH, HEADS], [0, DH]], channel_multiplier=-1).then_inc(consts, 1)

            def outer_product(b, t):
                g = T * b + t
                wait(pool, qkv_done, g + 1)
                wait(pool, run_done, g + 1 - T)
                k = qkv[:, t, D:2 * D].rearrange("p (h a) -> p h a", h=HEADS).unsqueeze(3).to_broadcast([P, HEADS, DH, DH])
                v = qkv[:, t, 2 * D:3 * D].rearrange("p (h b) -> p h b", h=HEADS).unsqueeze(2).to_broadcast([P, HEADS, DH, DH])
                pool.tensor_tensor(outer[:, t, :].rearrange("p (h a b) -> p h a b", h=HEADS, a=DH), k, v,
                                   ALU.mult).then_inc(outer_done, 1)

            def take_slots(b, t):
                if t:
                    return
                wait(pool, slot_done, b + 1)
                for u in range(T):
                    wait(pool, dispatch_done[u], 16 * K * b)
                apart(pool)
                pool.tensor_copy(slot[:, :], slot_next[:, :]).then_inc(slots_taken, 1)

            def dispatch(b, t):
                wait(pool, slots_taken, b + 1)
                wait(pool, rows_done, K * (T * b + t + 1))
                wait(pool, dest_done, T * b + t + 1)
                apart(pool)
                for k in range(K):
                    pool.indirect_dma_start(
                        out=dispatched[:, :], out_offset=bass.IndirectOffsetOnAxis(ap=slot[:, t * K + k:t * K + k + 1], axis=0),
                        in_=rows[:, t, k, :], in_offset=None).then_inc(dispatch_done[t], 16)

            pool.wait_ge(w_att, 6 * 16)
            pool.wait_ge(consts, N_CONSTS)
            for b in range(B):
                seq = slice(b * T * D, (b + 1) * T * D)
                pool.wait_ge(x_in[b], 16)
                pool.tensor_tensor(x2_sb[:, seq].rearrange("p (t d) -> p t d", t=T), x_sb[:, seq].rearrange("p (t d) -> p t d", t=T),
                                   bo_bc[:, :].unsqueeze(1).to_broadcast([P, T, D]), ALU.add).then_inc(xb_done, 1)
            run_slots(pool, [(0, outer_product), (13, take_slots), (13, dispatch)], N, T)

            def send_back(i, t):
                wait(pool, y_done, G * i + t + 1)
                apart(pool)
                pool.indirect_dma_start(
                    out=returned[:, :], out_offset=bass.IndirectOffsetOnAxis(ap=xt[:, t, D:D + 1].bitcast(I32), axis=0),
                    in_=y_sb[:, t, :], in_offset=None,
                    bounds_check=K * TOKENS - 1, oob_is_err=False).then_inc(return_done[t], 16)

            with pool.Fori(0, BLOCKS // G) as i:
                for t in range(G):
                    send_back(i, t)

        @block.scalar
        def _(act):
            def normalize(b, t):
                g = T * b + t
                wait(act, T1_done, g + 1 - T)
                act.activation(xn[:, t, :], tile(x_sb, b, t), ACT.Identity, bias=norm_at(norm, b, t, 1),
                               scale=norm_at(norm, b, t, 0)).then_inc(xn_done, 1)

            def xnT_out(b, t):
                wait(act, T1_done, T * b + t + 1)
                wait(act, qkv_mm, T * b + t + 1 - T)
                act.activation(xnT[:, t, :], ps_T1, ACT.Identity).then_inc(xnT_done, 1)

            def qT_out(b, t):
                wait(act, qkv_mm, T * b + t + 1)
                wait(act, oT_mm, T * b + t + 1 - T)
                act.activation(qT[:, t, :], ps_qT, ACT.Identity, bias=bq_col[:, 0:1]).then_inc(qT_done, 1)

            def oT_out(b, t):
                wait(act, oT_mm, T * b + t + 1)
                wait(act, att_mm, T * b + t + 1 - T)
                act.activation(oT[:, t, :], ps_oT, ACT.Identity).then_inc(oT_done, 1)

            def deviation2(b, t):
                wait(act, stats2_done, T * b + t + 1)
                wait(act, rstd2_done, T * b + t + 1 - T)
                act.activation(std2[:, t:t + 1], mv2[:, t, 1:2], ACT.Sqrt, bias=eps[:, 0:1]).then_inc(std2_done, 1)

            def normalize2(b, t):
                wait(act, norm2_done, T * b + t + 1)
                wait(act, x2_done, T * b + t + 1)
                wait(act, T2_done, T * b + t + 1 - T)
                act.activation(xn2[:, t, :], tile(x2_sb, b, t), ACT.Identity, bias=norm_at(norm2, b, t, 1),
                               scale=norm_at(norm2, b, t, 0)).then_inc(xn2_done, 1)

            def rows_out(b, t):
                wait(act, dispatch_done[t], 16 * K * b)
                for k in range(K):
                    act.activation(rows[:, t, k, 0:D], tile(x2_sb, b, t), ACT.Identity, bias=norm_at(norm2, b, t, 1),
                                   scale=norm_at(norm2, b, t, 0)).then_inc(rows_done, 1)

            def xn2T_out(b, t):
                wait(act, T2_done, T * b + t + 1)
                wait(act, lg_mm, T * b + t + 1 - T)
                act.activation(xn2T[:, t, :], ps_T2, ACT.Identity).then_inc(xn2T_done, 1)

            def exponentials(b, t):
                if t == T - 1:
                    wait(act, shift_done, b + 1)
                    wait(act, topi_done, T * b)
                    wait(act, gsum_done, b)
                    act.activation(expd[:, :, :], shifted[:, :, :], ACT.Exp).then_inc(exp_done, 1)

            act.wait_ge(consts, N_CONSTS)
            act.wait_ge(stats_done, N)
            act.activation(std[:, :], mv[:, :, 1], ACT.Sqrt, bias=eps[:, 0:1]).then_inc(std_done, 1)
            act.wait_ge(norm_done, 1)
            act.wait_ge(w_att, 6 * 16)
            run_slots(act, [(11, exponentials), (9, normalize2), (2, qT_out), (1, xnT_out), (14, rows_out), (9, xn2T_out),
                            (7, deviation2), (0, normalize), (5, oT_out)], N, T)

            def xT_out(i, t):
                n = G * i + t
                wait(act, TX_done, n + 1)
                wait(act, z_mm, n + 1 - G)
                act.activation(xT[:, t, :], ps_x[t % 2], ACT.Identity).then_inc(xT_done, 1)

            def hT_out(i, t):
                n = G * i + t
                wait(act, TH_done, n + 1)
                wait(act, y_mm, n + 1 - G)
                act.activation(hT[:, t, :, :].rearrange("p c k -> p (c k)"), ps_h[t % 2], ACT.Relu).then_inc(hT_done, 1)

            run_slots(act, [(0, xT_out), (2, hT_out)], BLOCKS, G)

        @block.vector
        def _(dve):
            def qkv_out(b, t):
                g = T * b + t
                wait(dve, qkv_mm, g + 1)
                wait(dve, outer_done, g + 1 - T)
                wait(dve, kv_done, (T - 1) * b)
                dve.tensor_tensor(qkv[:, t, :], ps_qkv, bqkv_bc[:, :], ALU.add).then_inc(qkv_done, 1)

            def state_out(b, t):
                if t == 0:
                    return
                wait(dve, kv_done, (T - 1) * b + t)
                wait(dve, att_mm, T * b + t - 2)
                wait(dve, oT_mm, T * b + t + 1 - T)
                dve.tensor_tensor(state[:, t, :], ps_state, headmask[:, :], ALU.mult).then_inc(state_done, 1)

            def attend(b, t):
                g = T * b + t
                wait(dve, run_done, g + 1)
                wait(dve, o_done, g - 1)
                q = qkv[:, t, 0:D].rearrange("p (h a) -> p h a", h=HEADS).unsqueeze(3).to_broadcast([P, HEADS, DH, DH])
                run = ps_run[t % 2].rearrange("p u f -> p (u f)").rearrange("p (h a b) -> p h a b", h=HEADS, a=DH)
                dve.tensor_tensor(prod[:, t % 2, :].rearrange("p (h a b) -> p h a b", h=HEADS, a=DH), run, q,
                                  ALU.mult).then_inc(prod_done, 1)

            def attend_sum(b, t):
                g = T * b + t
                wait(dve, prod_done, g + 1)
                wait(dve, oT_mm, g + 1 - T)
                dve.tensor_reduce(o_sb[:, t, :].rearrange("p (h b) -> p h b", h=HEADS),
                                  prod[:, t % 2, :].rearrange("p (h a b) -> p h b a", h=HEADS, a=DH),
                                  AX_X, ALU.add).then_inc(o_done, 1)

            def add_residual(b, t):
                g = T * b + t
                wait(dve, att_mm, g + 1)
                dve.tensor_tensor(tile(x2_sb, b, t), ps_att, tile(x2_sb, b, t), ALU.add).then_inc(x2_done, 1)

            def stats2_out(b, t):
                g = T * b + t
                wait(dve, x2_done, g + 1)
                apart(dve)
                dve.bn_stats(stats2[:, t, :], tile(x2_sb, b, t)).then_inc(stats2_raw, 1)

            def mean2_out(b, t):
                g = T * b + t
                wait(dve, stats2_raw, g + 1)
                wait(dve, std2_done, g + 1 - T)
                apart(dve)
                dve.bn_aggr(mv2[:, t, :], stats2[:, t, :]).then_inc(stats2_done, 1)

            def scale2_out(b, t):
                g = T * b + t
                wait(dve, std2_done, g + 1)
                dve.reciprocal(norm_at(norm2, b, t, 0), std2[:, t:t + 1]).then_inc(rstd2_done, 1)

            def shift2_out(b, t):
                g = T * b + t
                wait(dve, rstd2_done, g + 1)
                dve.scalar_tensor_tensor(out=norm_at(norm2, b, t, 1), in0=mv2[:, t, 0:1], scalar=-1.0,
                                         in1=norm_at(norm2, b, t, 0), op0=ALU.mult, op1=ALU.mult).then_inc(norm2_done, 1)

            def destinations(b, t):
                wait(dve, dispatch_done[t], 16 * K * b)
                dve.tensor_scalar(rows[:, t, :, D:D + 1].bitcast(I32), dest_in[:, t, :].unsqueeze(2), dest_from[:, bass.ds(b, 1)], None,
                                  ALU.add).then_inc(dest_done, 1)

            def over_e(ap):
                return ap[:, :].unsqueeze(2).to_broadcast([P, T, E])

            def softmax_start(b, t):
                if t < T - 1:
                    return
                wait(dve, lg_mm, T * (b + 1))
                wait(dve, att_mm, T * b + t + 5, N)
                dve.tensor_reduce(gmax[:, :], ps_lg, AX_X, ALU.max).then_inc(gmax_done, 1)
                wait(dve, gmax_done, b + 1)
                dve.tensor_tensor(shifted[:, :, :], ps_lg, over_e(gmax), ALU.subtract).then_inc(shift_done, 1)

            def softmax_end(b, t):
                if t < T - 1:
                    return
                wait(dve, exp_done, b + 1)
                dve.tensor_reduce(gsum[:, :], expd[:, :, :], AX_X, ALU.add).then_inc(gsum_done, 1)
                for u in range(T):
                    dve.max(top[:, u, :], expd[:, u, :]).then_inc(top_done, 1)
                wait(dve, gsum_done, b + 1)
                dve.reciprocal(grec[:, :], gsum[:, :]).then_inc(grec_done, 1)
                for u in range(T):
                    wait(dve, top_done, T * b + u + 1)
                    apart(dve)
                    dve.max_index(top_i[:, u, :], top[:, u, :], expd[:, u, :]).then_inc(topi_done, 1)
                wait(dve, grec_done, b + 1)
                dve.tensor_tensor(chosen[:, bass.ds(T * b * K, T * K)].rearrange("p (t k) -> p t k", t=T), top[:, :, 0:K],
                                  grec[:, :].unsqueeze(2).to_broadcast([P, T, K]), ALU.mult).then_inc(chosen_done, 1)
                wait(dve, topi_done, T * (b + 1))
                dve.tensor_copy(top_f[:, :, :], top_i[:, :, 0:K]).then_inc(topf_done, 1)

            def count(b, t):
                if t < T - 1:
                    return
                wait(dve, topf_done, b + 1)
                dve.tensor_tensor(pick[:, :, :, :], top_f[:, :, :].unsqueeze(3).to_broadcast([P, T, K, E]),
                                  expert_no[:, :].unsqueeze(1).unsqueeze(1).to_broadcast([P, T, K, E]),
                                  ALU.is_equal).then_inc(pick_done, 1)
                wait(dve, pick_done, b + 1)
                wait(dve, place_mm, b)
                dve.tensor_tensor(picked[:, :, :], pick[:, :, 0, :], pick[:, :, 1, :], ALU.add).then_inc(picked_done, 1)

            def places(b, t):
                if t < T - 1:
                    return
                wait(dve, place_mm, b + 1)
                wait(dve, lg_mm, T * b + t + 3, N)
                wait(dve, att_mm, T * b + t + 7, N)
                dve.tensor_tensor(place[:, :, :], ps_place, region_of[:, :].unsqueeze(1).to_broadcast([P, T, E]),
                                  ALU.add).then_inc(place_done, 1)
                dve.tensor_reduce(picked_sum[:, :], picked[:, :, :].rearrange("p t e -> p e t"), AX_X, ALU.add).then_inc(psum_done, 1)
                wait(dve, place_done, b + 1)
                dve.tensor_tensor(place_of[:, :, :, :], pick[:, :, :, :], place[:, :, :].unsqueeze(2).to_broadcast([P, T, K, E]),
                                  ALU.mult).then_inc(placeof_done, 1)
                wait(dve, psum_done, b + 1)
                dve.tensor_tensor(picked_before[:, :], picked_before[:, :], picked_sum[:, :], ALU.add).then_inc(before_done, 1)
                wait(dve, placeof_done, b + 1)
                dve.tensor_reduce(slot_f[:, :, :], place_of[:, :, :, :], AX_X, ALU.add).then_inc(slotf_done, 1)
                wait(dve, before_done, b + 1)
                dve.tensor_copy(picked_before_h[:, :], picked_before[:, :]).then_inc(before_h_done, 1)
                wait(dve, slotf_done, b + 1)
                wait(dve, slots_taken, b)
                dve.tensor_copy(slot_next[:, :].rearrange("p (t k) -> p t k", t=T), slot_f[:, :, :]).then_inc(slot_done, 1)

            for b in range(B):
                dve.wait_ge(x_in[b], 16)
                for g in range(b * T, (b + 1) * T):
                    dve.bn_stats(stats[:, g, :], x_sb[:, g * D:(g + 1) * D]).then_inc(stats_raw, 1)
                for g in range(b * T, (b + 1) * T):
                    dve.wait_ge(stats_raw, g + 1)
                    dve.bn_aggr(mv[:, g, :], stats[:, g, :]).then_inc(stats_done, 1)
            dve.wait_ge(std_done, 1)
            norm_v = norm[:, :].rearrange("p (g w) -> p g w", w=2)
            dve.reciprocal(norm_v[:, :, 0], std[:, :]).then_inc(rstd_done, 1)
            dve.wait_ge(rstd_done, 1)
            dve.scalar_tensor_tensor(out=norm_v[:, :, 1], in0=mv[:, :, 0], scalar=-1.0, in1=norm_v[:, :, 0],
                                     op0=ALU.mult, op1=ALU.mult).then_inc(norm_done, 1)
            dve.wait_ge(w_att, 6 * 16)
            dve.wait_ge(consts, N_CONSTS)
            dve.wait_ge(xb_done, B)
            run_slots(dve, [(6, scale2_out), (3, attend_sum), (0, qkv_out), (1, state_out), (10, places), (8, softmax_start),
                            (4, add_residual), (6, shift2_out), (9, softmax_end), (9, count), (11, destinations),
                            (4, stats2_out), (2, attend), (4, mean2_out)], N, T)

            steps = 0

            def step(ins):
                nonlocal steps
                steps += 1
                ins.then_inc(table_step, 1)
                dve.wait_ge(table_step, steps)

            dve.wait_ge(cnt_mm, 1)
            dve.tensor_tensor(end_row[:, :], ps_cnt, region_of[0:1, :], ALU.add).then_inc(end_row_done, 1)
            step(dve.tensor_scalar(cnt_i[:, :], ps_cnt, float(P - 1), None, ALU.add))
            step(dve.tensor_scalar(cnt_i[:, :], cnt_i[:, :], P.bit_length() - 1, None, ALU.arith_shift_right))
            step(dve.tensor_copy(n_blocks[:, :], cnt_i[:, :]))
            step(dve.tensor_tensor_scan(end_block[:, :], one_row[:, :], n_blocks[:, :], 0.0, ALU.mult, ALU.add))
            dve.tensor_tensor(past[:, :, :], block_no[:, :].unsqueeze(2).to_broadcast([1, BLOCKS, E]),
                              end_block[:, :].unsqueeze(1).to_broadcast([1, BLOCKS, E]), ALU.is_ge).then_inc(table_step, 1)
            dve.tensor_scalar(jump[:, :], n_blocks[:, :], -float(P), float(REGION), ALU.mult, ALU.add).then_inc(table_step, 1)
            steps += 1
            dve.wait_ge(table_step, steps)
            dve.tensor_reduce(expert_f[:, :], past[:, :, :], AX_X, ALU.add).then_inc(table_step, 1)
            steps += 1
            dve.wait_ge(table_step, steps)
            dve.tensor_tensor(skipped[:, :, :], past[:, :, :], jump[:, :].unsqueeze(1).to_broadcast([1, BLOCKS, E]),
                              ALU.mult).then_inc(table_step, 1)
            steps += 1
            dve.wait_ge(table_step, steps)
            dve.tensor_scalar(w1_at[:, HIDDEN:HIDDEN + BLOCKS], expert_f[:, :], float(E - 1), float(H), ALU.min, ALU.mult).then_inc(table_done, 1)
            dve.tensor_scalar(w2_at[:, OUTPUT:OUTPUT + BLOCKS], expert_f[:, :], float(E - 1), float(D), ALU.min, ALU.mult).then_inc(table_done, 1)
            steps += 1
            dve.wait_ge(table_step, steps)
            step(dve.tensor_reduce(row_f[:, :], skipped[:, :, :], AX_X, ALU.add))
            step(dve.tensor_tensor(row_f[:, :], row_f[:, :], block_row[:, :], ALU.add))
            dve.tensor_scalar(row_at[:, :], row_f[:, :], float(PAD_BLOCK), None, ALU.min).then_inc(table_done, 1)

            dve.wait_ge(table_done, 2)
            dve.wait_ge(w_ffn, (3 + HC) * 16)

            at = {}

            def experts_of_group(i):
                at[HIDDEN] = read(mybir.EngineType.DVE, w1_at[0:1, bass.ds(G * i, G)], (E - 1) * H)
                at[OUTPUT] = read(mybir.EngineType.DVE, w2_at[0:1, bass.ds(G * i, G)], (E - 1) * D)

            def z_out(i, t):
                n = G * i + t
                wait(dve, z_mm, n + 1)
                wait(dve, TH_done, n + 1 - G)
                dve.tensor_tensor(z_sb[:, t, :], ps_z[t % 2], b1_bc[:, bass.ds(at[HIDDEN][(t + HIDDEN) % G], H)], ALU.add).then_inc(z_done, 1)

            def y_out(i, t):
                n = G * i + t
                wait(dve, y_mm, n + 1)
                wait(dve, return_done[t], 16 * i)
                dve.tensor_tensor(y_sb[:, t, :], ps_y[t % 2], b2_bc[:, bass.ds(at[OUTPUT][(t + OUTPUT) % G], D)], ALU.add).then_inc(y_done, 1)

            run_slots(dve, [(HIDDEN, z_out), (OUTPUT, y_out)], BLOCKS, G, experts_of_group)

            for b in range(B):
                dve.wait_ge(back_in[b], 16)
                for k in range(K):
                    for t in range(T):
                        g = T * b + t
                        if k:
                            dve.wait_ge(first_added, g + 1)
                        dst = x2_sb[:, g * D:(g + 1) * D]
                        dve.scalar_tensor_tensor(out=dst, in0=back[:, (g * K + k) * D:(g * K + k + 1) * D],
                                                 scalar=chosen[:, g * K + k:g * K + k + 1], in1=dst,
                                                 op0=ALU.mult, op1=ALU.add).then_inc(both_added if k else first_added, 1)

        @block.tensor
        def _(pe):
            def transpose1(b, t):
                g = T * b + t
                wait(pe, xn_done, g + 1)
                wait(pe, oT_done, g - 4)
                pe.transpose(ps_T1, xn[:, t, :], ident[:, :]).then_inc(T1_done, 1)

            def project(b, t):
                g = T * b + t
                wait(pe, xnT_done, g + 1)
                wait(pe, xn2T_done, g - 7)
                wait(pe, qkv_done, g)
                pe.matmul(ps_qT, wqkv_sb[:, 0:D], xnT[:, t, :], start=True, stop=True)
                pe.matmul(ps_qkv, xnT[:, t, :], wqkv_sb[:, :], start=True, stop=True).then_inc(qkv_mm, 1)

            def running_sums(b, t):
                g = T * b + t
                wait(pe, outer_done, g + 1)
                wait(pe, prod_done, g - 1)
                for u in range(2):
                    mm = pe.matmul(ps_run[t % 2][:, u, :], causal[:, :], outer[:, t, 512 * u:512 * (u + 1)],
                                   start=True, stop=True)
                mm.then_inc(run_done, 1)

            def sum_state(b, t):
                if t == 0:
                    return
                wait(pe, qkv_done, T * b + t)
                wait(pe, state_done, (T - 1) * b + t - 1)
                wait(pe, x2_done, T * b + t - 3)
                for u in range(t):
                    mm = pe.matmul(ps_state, qkv[:, u, D:2 * D], qkv[:, u, 2 * D:3 * D], start=(u == 0), stop=(u == t - 1))
                mm.then_inc(kv_done, 1)

            def o_transposed(b, t):
                g = T * b + t
                wait(pe, o_done, g + 1)
                wait(pe, xnT_done, g + 5, N)
                wait(pe, oT_done, g)
                mm = pe.matmul(ps_oT, o_sb[:, t, :], ident[:, :], start=True, stop=(t == 0))
                if t:
                    wait(pe, state_done, (T - 1) * b + t)
                    wait(pe, qT_done, g + 1)
                    mm = pe.matmul(ps_oT, state[:, t, :], qT[:, t, :], start=False, stop=True)
                mm.then_inc(oT_mm, 1)

            def project_out(b, t):
                g = T * b + t
                wait(pe, oT_done, g + 1)
                wait(pe, x2_done, g)
                wait(pe, state_done, (T - 1) * b + min(t + 2, T - 1) + (t == T - 1), (T - 1) * B)
                pe.matmul(ps_att, oT[:, t, :], wo_sb[:, :], start=True, stop=True).then_inc(att_mm, 1)

            def transpose2(b, t):
                g = T * b + t
                wait(pe, xn2_done, g + 1)
                wait(pe, qT_done, g + 8, N)
                wait(pe, xn2T_done, g)
                pe.transpose(ps_T2, xn2[:, t, :], ident[:, :]).then_inc(T2_done, 1)

            def gate(b, t):
                wait(pe, xn2T_done, T * b + t + 1)
                wait(pe, x2_done, T * b + t + 4, N)
                if t == 0:
                    wait(pe, shift_done, b)
                if t == 2:
                    wait(pe, place_done, b)
                pe.matmul(ps_lg[:, t, :], xn2T[:, t, :], wg_sb[:, :], start=True, stop=True).then_inc(lg_mm, 1)

            def rank(b, t):
                if t < T - 1:
                    return
                wait(pe, picked_done, b + 1)
                wait(pe, x2_done, T * b + t + 6, N)
                wait(pe, before_h_done, b)
                pe.matmul(ps_place, earlier[:, :], picked[:, :, :], start=True, stop=False, skip_group_check=True)
                for u in range(T - 1):
                    pe.matmul(ps_place[:, u + 1:T, :], ones[:, :],
                              picked[:, u, :].unsqueeze(1).to_broadcast([P, T - 1 - u, E]),
                              start=False, stop=False, skip_group_check=True)
                mm = pe.matmul(ps_place, ones[:, :], picked_before_h[:, :].unsqueeze(1).to_broadcast([P, T, E]),
                               start=False, stop=True, skip_group_check=True)
                mm.then_inc(place_mm, 1)

            pe.wait_ge(consts, N_CONSTS)
            pe.wait_ge(w_att, 6 * 16)
            run_slots(pe, [(1, project), (0, transpose1), (2, sum_state), (9, gate), (11, rank), (5, project_out),
                           (8, transpose2), (3, running_sums), (4, o_transposed)], N, T)

            pe.wait_ge(before_h_done, B)
            pe.matmul(ps_cnt, ones[:, 0:1], picked_before_h[:, :], start=True, stop=True).then_inc(cnt_mm, 1)

            pe.wait_ge(table_done, 2)
            pe.wait_ge(w_ffn, (3 + HC) * 16)

            at = {}

            def experts_of_group(i):
                at[HIDDEN] = read(mybir.EngineType.PE, w1_at[0:1, bass.ds(G * i, G)], (E - 1) * H)
                at[OUTPUT] = read(mybir.EngineType.PE, w2_at[0:1, bass.ds(G * i, G)], (E - 1) * D)

            def transpose_x(i, t):
                n = G * i + t
                pe.wait_ge(xt_in[t], 16 * (i + 1))
                wait(pe, xT_done, n - 1)
                pe.transpose(ps_x[t % 2], xt[:, t, 0:D], ident[:, :]).then_inc(TX_done, 1)

            def hidden(i, t):
                n = G * i + t
                wait(pe, xT_done, n + 1)
                wait(pe, z_done, n - 1)
                pe.matmul(ps_z[t % 2], xT[:, t, :], w1_sb[:, bass.ds(at[HIDDEN][(t + HIDDEN) % G], H)], start=True, stop=True).then_inc(z_mm, 1)

            def transpose_h(i, t):
                n = G * i + t
                wait(pe, z_done, n + 1)
                wait(pe, hT_done, n - 1)
                for c in range(HC):
                    mm = pe.transpose(ps_h[t % 2][:, c * P:(c + 1) * P], z_sb[:, t, c * P:(c + 1) * P], ident[:, :])
                mm.then_inc(TH_done, 1)

            def output(i, t):
                n = G * i + t
                wait(pe, hT_done, n + 1)
                wait(pe, y_done, n - 1)
                for c in range(HC):
                    mm = pe.matmul(ps_y[t % 2], hT[:, t, c, :], w2_sb[:, c, bass.ds(at[OUTPUT][(t + OUTPUT) % G], D)], start=(c == 0), stop=(c == HC - 1))
                mm.then_inc(y_mm, 1)

            run_slots(pe, [(0, transpose_x), (HIDDEN, hidden), (2, transpose_h), (OUTPUT, output)], BLOCKS, G, experts_of_group)


_OUT = (8, 512, 128)


def kernel(L0_attn_x, L0_attn_wq_w, L0_attn_wq_b, L0_attn_wk_w, L0_attn_wk_b, L0_attn_wv_w, L0_attn_wv_b,
           L0_attn_wo_w, L0_attn_wo_b, L0_ffn_Wg, L0_ffn_W1, L0_ffn_b1, L0_ffn_W2, L0_ffn_b2):
    import numpy as np
    import concourse.bacc as bacc
    from concourse.bass_utils import run_bass_kernel_spmd

    arrays = {
        "x": L0_attn_x,
        "w_qkv": np.concatenate([np.asarray(w).T for w in (L0_attn_wq_w, L0_attn_wk_w, L0_attn_wv_w)], axis=1),
        "b_qkv": np.concatenate([np.asarray(b) for b in (L0_attn_wq_b, L0_attn_wk_b, L0_attn_wv_b)]),
        "b_q": np.asarray(L0_attn_wq_b).reshape(-1, 1),
        "w_o": np.asarray(L0_attn_wo_w).T,
        "b_o": L0_attn_wo_b,
        "w_gate": L0_ffn_Wg,
        "w1": L0_ffn_W1,
        "b1": np.asarray(L0_ffn_b1).reshape(-1),
        "w2": L0_ffn_W2,
        "b2": np.asarray(L0_ffn_b2).reshape(-1),
    }
    arrays = {name: np.ascontiguousarray(a) for name, a in arrays.items()}
    nc = bacc.Bacc("TRN2", target_bir_lowering=False, num_devices=1)
    args = {name: nc.dram_tensor(name, a.shape, mybir.dt.from_np(a.dtype), kind="ExternalInput").ap()
            for name, a in arrays.items()}
    out = nc.dram_tensor("out", _OUT, F32, kind="ExternalOutput").ap()
    preln_linear_attention_moe(nc, out=out, **args)
    result = run_bass_kernel_spmd(nc, [arrays], core_ids=[0])
    return result.results[0]["out"]
```

```python
from contextlib import ExitStack

import concourse.bass as bass
from concourse import mybir

ALU = mybir.AluOpType
ACT = mybir.ActivationFunctionType
AX_X = mybir.AxisListType.X
F32 = mybir.dt.float32
BF16 = mybir.dt.bfloat16
I32 = mybir.dt.int32
U32 = mybir.dt.uint32

P = 128
HEADS = 16
DH = P // HEADS
EPS = 1e-5


def wait(eng, sem, value, most=None):
    if isinstance(value, int):
        value = value if most is None else min(value, most)
        if value <= 0:
            return
    eng.wait_ge(sem, value)


def run_slots(eng, stages, n_tiles, group, at_group=None, at_slot=None):
    deepest = max(lag for lag, _ in stages)
    first = -(-deepest // group) * group + group
    for s in range(first):
        if at_group and s % group == 0:
            at_group(s // group)
        for lag, stage in stages:
            if s >= lag:
                stage((s - lag) // group, (s - lag) % group)
        if at_slot:
            at_slot(s)
    with eng.Fori(first // group, n_tiles // group) as i:
        if at_group:
            at_group(i)
        for t in range(group):
            for lag, stage in stages:
                stage(i + (t - lag) // group, (t - lag) % group)
    for s in range(n_tiles, n_tiles + deepest):
        if at_group and s % group == 0:
            at_group(s // group)
        for lag, stage in stages:
            if s - lag < n_tiles:
                stage((s - lag) // group, (s - lag) % group)


def preln_linear_attention_moe(nc, x, w_qkv, b_qkv, b_q, w_o, b_o, w_gate, w1, b1, w2, b2, out):
    B, L, D = x.shape
    E, _, H = w1.shape
    T = L // P
    N = B * T
    TOKENS = N * P
    HC = H // P
    OUTER = D * DH
    K = 2
    ROW = D + 4
    REGION = TOKENS + P
    PAD_BLOCK = E * REGION
    NOWHERE = K * TOKENS
    G = 12
    W = 4
    HIDDEN, OUTPUT = 1, 2
    BLOCKS = -(-((K * TOKENS + E * (P - 1)) // P) // G) * G
    AHEAD = [range(T), range(T, N)]
    assert D == P and T == 4 and H == HC * P

    with ExitStack() as ctx:
        def sb(name, shape, dt=F32):
            return ctx.enter_context(nc.sbuf_tensor(name, shape, dt))

        def sem(name):
            return ctx.enter_context(nc.semaphore(name))

        dispatched = nc.dram_tensor("dispatched", [PAD_BLOCK + P, ROW], F32, kind="Internal").ap()
        returned = nc.dram_tensor("returned", [K * TOKENS, D], F32, kind="Internal").ap()

        ident = sb("ident", [P, P])
        causal = sb("causal", [P, P])
        earlier = sb("earlier", [P, P], BF16)
        ones = sb("ones", [P, P], BF16)
        headmask = sb("headmask", [P, P])
        eps = sb("eps", [P, 1])
        first_root = sb("first_root", [P, 1])
        dest_in = sb("dest_in", [P, T, K])
        dest_from = sb("dest_from", [P, B])
        expert_no = sb("expert_no", [P, E])
        region_of = sb("region_of", [P, E])
        block_no = sb("block_no", [1, BLOCKS])
        block_row = sb("block_row", [1, BLOCKS])
        padding = sb("padding", [P, ROW])
        wqkv_sb = sb("wqkv_sb", [P, 3 * D])
        bqkv_bc = sb("bqkv_bc", [P, 3 * D])
        bias_high = sb("bias_high", [P, 3 * D], BF16)
        bias_rest = sb("bias_rest", [P, 3 * D])
        bias_middle = sb("bias_middle", [P, 3 * D], BF16)
        bias_parts = sb("bias_parts", [P, 3 * D], BF16)
        bq_col = sb("bq_col", [P, 1])
        wo_sb = sb("wo_sb", [P, D])
        bo_bc = sb("bo_bc", [P, D])
        wg_sb = sb("wg_sb", [P, E])
        w1_sb = sb("w1_sb", [P, E * H])
        b1_col = sb("b1_col", [P, E * HC])
        w2_sb = sb("w2_sb", [P, HC, E * D])
        b2_bc = sb("b2_bc", [P, E * D])
        x_sb = sb("x_sb", [P, N * D])
        x2_sb = sb("x2_sb", [P, N * D])
        stats = sb("stats", [P, N, 6])
        mv = sb("mv", [P, N, 2])
        std = sb("std", [P, N])
        norm = sb("norm", [P, N * 2])
        back = sb("back", [P, N * K * D])
        chosen = sb("chosen", [P, N * K])
        xn = sb("xn", [P, T, D])
        xnT = sb("xnT", [P, T, P])
        qT = sb("qT", [P, T, P])
        qkv = sb("qkv", [P, T, 3 * D])
        outer = sb("outer", [P, T, OUTER])
        state = sb("state", [P, T, D])
        prod = sb("prod", [P, 2, OUTER])
        o_sb = sb("o_sb", [P, T, D])
        oT = sb("oT", [P, T, P])
        stats2 = sb("stats2", [P, T, 6])
        mv2 = sb("mv2", [P, T, 2])
        std2 = sb("std2", [P, T])
        norm2 = sb("norm2", [P, N * 2])
        xn2 = sb("xn2", [P, T, D])
        rows = sb("rows", [P, T, K, ROW])
        xn2T = sb("xn2T", [P, T, P])
        gmax = sb("gmax", [P, T])
        shifted = sb("shifted", [P, T, E])
        expd = sb("expd", [P, T, E])
        gsum = sb("gsum", [P, T])
        grec = sb("grec", [P, T])
        top = sb("top", [P, T, E])
        top_i = sb("top_i", [P, T, E], U32)
        top_f = sb("top_f", [P, T, K])
        pick = sb("pick", [P, T, K, E])
        picked = sb("picked", [P, T, E], BF16)
        picked_sum = sb("picked_sum", [P, E])
        picked_before = sb("picked_before", [P, E])
        picked_before_h = sb("picked_before_h", [P, E], BF16)
        place = sb("place", [P, T, E])
        place_of = sb("place_of", [P, T, K, E])
        slot_f = sb("slot_f", [P, T, K])
        slot_next = sb("slot_next", [P, T * K], I32)
        slot = sb("slot", [P, T * K], I32)
        cnt_i = sb("cnt_i", [1, E], I32)
        end_row = sb("end_row", [1, E], I32)
        n_blocks = sb("n_blocks", [1, E])
        one_row = sb("one_row", [1, E])
        end_block = sb("end_block", [1, E])
        jump = sb("jump", [1, E])
        past = sb("past", [1, BLOCKS, E])
        skipped = sb("skipped", [1, BLOCKS, E])
        row_f = sb("row_f", [1, BLOCKS])
        expert_f = sb("expert_f", [1, BLOCKS])
        row_at = sb("row_at", [1, BLOCKS], I32)
        w1_at = sb("w1_at", [1, BLOCKS + G], I32)
        b1_at = sb("b1_at", [1, BLOCKS + G], I32)
        w2_at = sb("w2_at", [1, BLOCKS + G], I32)
        xt = sb("xt", [P, G, ROW])
        xT = sb("xT", [P, G, P])
        w1_of = sb("w1_of", [P, W, H])
        hT = sb("hT", [P, G, HC, P])
        y_sb = sb("y_sb", [P, G, D])

        ps = ctx.enter_context(nc.psum_tensor("ps", [P, 8, 512], F32))
        ps_T1 = ps[:, 0, 0:P]
        ps_oT = ps[:, 0, P:2 * P]
        ps_qT = ps[:, 1, 0:P]
        ps_T2 = ps[:, 1, P:2 * P]
        ps_run = [ps[:, 2:4, :], ps[:, 4:6, :]]
        ps_qkv = ps[:, 6, 0:3 * D]
        ps_state = ps[:, 7, 0:D]
        ps_att = ps[:, 7, P:2 * P]
        ps_lg = ps[:, 7, 2 * P:2 * P + T * E].rearrange("p (t e) -> p t e", t=T)
        ps_place = ps[:, 7, 3 * P:3 * P + T * E].rearrange("p (t e) -> p t e", t=T)
        ps_cnt = ps[0:1, 7, 3 * P + T * E:3 * P + T * E + E]
        ps_x = [ps[:, u, 0:P] for u in range(2)]
        ps_h = [ps[:, 2 + u, 0:H] for u in range(2)]
        ps_y = [ps[:, 4 + u, 0:D] for u in range(2)]

        consts, passed = sem("consts"), sem("passed")
        x_in = [sem(f"x_in{b}") for b in range(B)]
        w_att, w_ffn = sem("w_att"), sem("w_ffn")
        bias_in, parts_cleared, bias_step, bias_done = sem("bias_in"), sem("parts_cleared"), sem("bias_step"), sem("bias_done")
        eps_done, root_done = sem("eps_done"), sem("root_done")
        stats_raw, stats_done, std_done, rstd_done, norm_done = sem("stats_raw"), sem("stats_done"), sem("std_done"), sem("rstd_done"), sem("norm_done")
        xn_done, T1_done, xnT_done = sem("xn_done"), sem("T1_done"), sem("xnT_done")
        qkv_mm, qT_done, qkv_done = sem("qkv_mm"), sem("qT_done"), sem("qkv_done")
        outer_done, run_done, kv_done, state_done = sem("outer_done"), sem("run_done"), sem("kv_done"), sem("state_done")
        prod_done, o_done, oT_mm, oT_done = sem("prod_done"), sem("o_done"), sem("oT_mm"), sem("oT_done")
        att_mm, xb_done, x2_done = sem("att_mm"), sem("xb_done"), sem("x2_done")
        stats2_raw, stats2_done, std2_done, rstd2_done, norm2_done = (
            sem("stats2_raw"), sem("stats2_done"), sem("std2_done"), sem("rstd2_done"), sem("norm2_done"))
        xn2_done, rows_done, T2_done, xn2T_done = sem("xn2_done"), sem("rows_done"), sem("T2_done"), sem("xn2T_done")
        lg_mm = sem("lg_mm")
        gmax_done, shift_done, exp_done, gsum_done = sem("gmax_done"), sem("shift_done"), sem("exp_done"), sem("gsum_done")
        grec_done, top_done, topi_done, topf_done = sem("grec_done"), sem("top_done"), sem("topi_done"), sem("topf_done")
        chosen_done, pick_done, picked_done, place_mm = sem("chosen_done"), sem("pick_done"), sem("picked_done"), sem("place_mm")
        psum_done, before_done, before_h_done = sem("psum_done"), sem("before_done"), sem("before_h_done")
        place_done, placeof_done, slotf_done, slot_done = sem("place_done"), sem("placeof_done"), sem("slotf_done"), sem("slot_done")
        slots_taken = sem("slots_taken")
        dispatch_done = [sem(f"dispatch_done{t}") for t in range(T)]
        cnt_mm, table_step, end_row_done, table_done, pads_done = sem("cnt_mm"), sem("table_step"), sem("end_row_done"), sem("table_done"), sem("pads_done")
        xt_in = [sem(f"xt_in{t}") for t in range(G)]
        TX_done, xT_done, w1_done, h_mm, hT_done, y_mm, y_done = (
            sem("TX_done"), sem("xT_done"), sem("w1_done"), sem("h_mm"), sem("hT_done"), sem("y_mm"), sem("y_done"))
        dest_done = sem("dest_done")
        return_done = [sem(f"return_done{t}") for t in range(G)]
        back_in = [sem(f"back_in{b}") for b in range(B)]
        first_added, second_scaled, both_added = sem("first_added"), sem("second_scaled"), sem("both_added")
        stored = sem("stored")

        def tile(buf, b, t):
            return buf[:, bass.ds((T * b + t) * P, P)]

        def norm_at(buf, b, t, w):
            return buf[:, bass.ds((T * b + t) * 2 + w, 1)]

        def bcast(ap):
            return ap.partition_broadcast(P)

        x_t = x.rearrange("b (t p) d -> b p t d", p=P)
        out_t = out.rearrange("b (t p) d -> b p t d", p=P)
        back_t = returned.rearrange("(b t p k) d -> b p t (k d)", b=B, t=T, k=K)

        N_FILLS = 13
        N_CONSTS = N_FILLS + 12
        block = ctx.enter_context(nc.Block())

        def apart(eng):
            eng.sem_inc(passed, 1)

        def read(engine, numbers, most):
            return nc.values_load_multi_w_load_instructions(
                numbers, engines=[engine], min_val=0, max_val=most,
                skip_runtime_bounds_check_because="the table's steps bound them")[1]

        @block.sync
        def _(sp):
            def load_x(b):
                return sp.dma_start(x_sb[:, b * T * D:(b + 1) * T * D].rearrange("p (t d) -> p t d", t=T), x_t[b])
            load_x(0).then_inc(x_in[0], 16)
            sp.dma_start(bqkv_bc[:, :], bcast(b_qkv)).then_inc(bias_in, 16)
            sp.dma_start(wqkv_sb[:, :], w_qkv).then_inc(w_att, 16)
            sp.dma_start(bq_col[:, :], b_q).then_inc(w_att, 16)
            sp.dma_start(wo_sb[:, :], w_o).then_inc(w_att, 16)
            sp.dma_start(bo_bc[:, :], bcast(b_o)).then_inc(w_att, 16)
            sp.dma_start(wg_sb[:, :], w_gate).then_inc(w_att, 16)
            for b in range(1, B):
                load_x(b).then_inc(x_in[b], 16)
            sp.dma_start(w1_sb[:, :].rearrange("d (e h) -> d e h", e=E), w1.rearrange("e d h -> d e h")).then_inc(w_ffn, 16)
            sp.dma_start(b1_col[:, :], b1).then_inc(w_ffn, 16)
            for c in range(HC):
                sp.dma_start(w2_sb[:, c, :].rearrange("p (e d) -> p e d", e=E),
                             w2[:, c * P:(c + 1) * P, :].rearrange("e p d -> p e d")).then_inc(w_ffn, 16)
            sp.dma_start(b2_bc[:, :], bcast(b2)).then_inc(w_ffn, 16)
            sp.wait_ge(consts, N_CONSTS)
            sp.dma_start(dispatched[PAD_BLOCK:PAD_BLOCK + P, :], padding[:, :]).then_inc(pads_done, 16)

            sp.wait_ge(end_row_done, 1)
            for row in read(mybir.EngineType.SP, end_row[0:1, 0:E], PAD_BLOCK):
                sp.dma_start(dispatched[bass.ds(row, P), :], padding[:, :]).then_inc(pads_done, 16)
            sp.wait_ge(table_done, 4)
            sp.wait_ge(pads_done, 16 * (E + 1))
            for t in range(T):
                sp.wait_ge(dispatch_done[t], 16 * B * K)

            def load_block(i, t, row):
                wait(sp, TX_done, G * (i - 1) + t + 1)
                apart(sp)
                wait(sp, return_done[t], 16 * i)
                apart(sp)
                sp.dma_start(xt[:, t, :], dispatched[bass.ds(row, P), :]).then_inc(xt_in[t], 16)

            rows_at = read(mybir.EngineType.SP, row_at[0:1, 0:G], PAD_BLOCK)
            for t in range(G):
                load_block(0, t, rows_at[t])
            with sp.Fori(1, BLOCKS // G) as i:
                rows_at = read(mybir.EngineType.SP, row_at[0:1, bass.ds(G * i, G)], PAD_BLOCK)
                for t in range(G):
                    load_block(i, t, rows_at[t])

            for t in range(G):
                sp.wait_ge(return_done[t], 16 * (BLOCKS // G))
            for b in range(B):
                sp.dma_start(back[:, b * T * K * D:(b + 1) * T * K * D].rearrange("p (t f) -> p t f", t=T),
                             back_t[b]).then_inc(back_in[b], 16)
            for b in range(B):
                sp.wait_ge(both_added, b + 1)
                sp.dma_start(out_t[b], x2_sb[:, b * T * D:(b + 1) * T * D].rearrange("p (t d) -> p t d", t=T)).then_inc(stored, 16)
            sp.wait_ge(stored, 16 * B)

        @block.gpsimd
        def _(pool):
            pool.memset(eps[:, :], EPS).then_inc(eps_done, 1)
            pool.memset(bias_parts[:, :], 0.0).then_inc(parts_cleared, 1)
            pool.memset(ident[:, :], 0.0).then_inc(consts, 1)
            pool.memset(causal[:, :], 1.0).then_inc(consts, 1)
            pool.memset(earlier[:, :], 1.0).then_inc(consts, 1)
            pool.memset(ones[:, :], 1.0).then_inc(consts, 1)
            pool.memset(headmask[:, :], 1.0).then_inc(consts, 1)
            pool.memset(padding[:, :], 0.0).then_inc(consts, 1)
            pool.memset(picked_before[:, :], 0.0).then_inc(consts, 1)
            pool.iota(expert_no[:, :], pattern=[[1, E]], base=0, channel_multiplier=0,
                      allow_small_or_imprecise_dtypes=True).then_inc(consts, 1)
            pool.iota(region_of[:, :], pattern=[[REGION, E]], base=0, channel_multiplier=0,
                      allow_small_or_imprecise_dtypes=True).then_inc(consts, 1)
            pool.iota(block_no[:, :], pattern=[[1, BLOCKS]], base=0, channel_multiplier=0,
                      allow_small_or_imprecise_dtypes=True).then_inc(consts, 1)
            pool.iota(dest_in[:, :, :], pattern=[[P * K, T], [1, K]], base=0, channel_multiplier=K,
                      allow_small_or_imprecise_dtypes=True).then_inc(consts, 1)
            pool.iota(dest_from[:, :], pattern=[[T * P * K, B]], base=0, channel_multiplier=0,
                      allow_small_or_imprecise_dtypes=True).then_inc(consts, 1)
            pool.memset(rows[:, :, :, :], 0.0).then_inc(consts, 1)
            pool.wait_ge(consts, N_FILLS)
            pool.affine_select(out=ident[:, :], in_=ident[:, :], compare_op=ALU.not_equal, fill=1.0,
                               base=0, pattern=[[-1, P]], channel_multiplier=1).then_inc(consts, 1)
            pool.affine_select(out=causal[:, :], in_=causal[:, :], compare_op=ALU.is_ge, fill=0.0,
                               base=0, pattern=[[1, P]], channel_multiplier=-1).then_inc(consts, 1)
            pool.affine_select(out=earlier[:, :], in_=earlier[:, :], compare_op=ALU.is_ge, fill=0.0,
                               base=-1, pattern=[[1, P]], channel_multiplier=-1).then_inc(consts, 1)
            hm = headmask[:, :].rearrange("p (h a) -> p h a", h=HEADS)
            pool.affine_select(out=hm, in_=hm, compare_op=ALU.is_ge, fill=0.0,
                               base=0, pattern=[[-DH, HEADS], [0, DH]], channel_multiplier=1).then_inc(consts, 1)
            pool.iota(padding[:, D:ROW].bitcast(I32), pattern=[[0, ROW - D]], base=NOWHERE, channel_multiplier=0).then_inc(consts, 1)
            pool.iota(block_row[:, :], pattern=[[P, BLOCKS]], base=0, channel_multiplier=0,
                      allow_small_or_imprecise_dtypes=True).then_inc(consts, 1)
            pool.memset(one_row[:, :], 1.0).then_inc(consts, 1)
            pool.memset(picked_before_h[:, :], 0.0).then_inc(consts, 1)
            pool.memset(w1_at[:, :], 0).then_inc(consts, 1)
            pool.memset(b1_at[:, :], 0).then_inc(consts, 1)
            pool.memset(w2_at[:, :], 0).then_inc(consts, 1)
            pool.wait_ge(consts, N_FILLS + 11)
            pool.affine_select(out=hm, in_=hm, compare_op=ALU.is_ge, fill=0.0,
                               base=DH - 1, pattern=[[DH, HEADS], [0, DH]], channel_multiplier=-1).then_inc(consts, 1)

            def outer_product(b, t):
                g = T * b + t
                wait(pool, qkv_done, g + 1)
                wait(pool, run_done, g + 1 - T)
                k = qkv[:, t, D:2 * D].rearrange("p (h a) -> p h a", h=HEADS).unsqueeze(3).to_broadcast([P, HEADS, DH, DH])
                v = qkv[:, t, 2 * D:3 * D].rearrange("p (h b) -> p h b", h=HEADS).unsqueeze(2).to_broadcast([P, HEADS, DH, DH])
                pool.tensor_tensor(outer[:, t, :].rearrange("p (h a b) -> p h a b", h=HEADS, a=DH), k, v,
                                   ALU.mult).then_inc(outer_done, 1)

            def take_slots(b, t):
                if t % 2:
                    return
                wait(pool, slot_done, b + 1)
                wait(pool, dispatch_done[t], 16 * K * b)
                wait(pool, dispatch_done[t + 1], 16 * K * b)
                apart(pool)
                pool.tensor_copy(slot[:, t * K:(t + 2) * K], slot_next[:, t * K:(t + 2) * K]).then_inc(slots_taken, 1)

            def dispatch(b, t):
                wait(pool, slots_taken, T // 2 * b + t // 2 + 1)
                wait(pool, rows_done, K * (T * b + t + 1))
                wait(pool, dest_done, T * b + t + 1)
                apart(pool)
                for k in range(K):
                    pool.indirect_dma_start(
                        out=dispatched[:, :], out_offset=bass.IndirectOffsetOnAxis(ap=slot[:, t * K + k:t * K + k + 1], axis=0),
                        in_=rows[:, t, k, :], in_offset=None).then_inc(dispatch_done[t], 16)

            pool.wait_ge(w_att, 5 * 16)
            pool.wait_ge(consts, N_CONSTS)

            def add_bias(b):
                if b >= B:
                    return
                seq = slice(b * T * D, (b + 1) * T * D)
                pool.wait_ge(x_in[b], 16)
                pool.tensor_tensor(x2_sb[:, seq].rearrange("p (t d) -> p t d", t=T), x_sb[:, seq].rearrange("p (t d) -> p t d", t=T),
                                   bo_bc[:, :].unsqueeze(1).to_broadcast([P, T, D]), ALU.add).then_inc(xb_done, 1)
            run_slots(pool, [(0, outer_product), (13, take_slots), (13, dispatch)], N, T, at_slot=add_bias)

            def send_back(i, t):
                wait(pool, y_done, G * i + t + 1)
                apart(pool)
                pool.indirect_dma_start(
                    out=returned[:, :], out_offset=bass.IndirectOffsetOnAxis(ap=xt[:, t, D:D + 1].bitcast(I32), axis=0),
                    in_=y_sb[:, t, :], in_offset=None,
                    bounds_check=K * TOKENS - 1, oob_is_err=False).then_inc(return_done[t], 16)

            with pool.Fori(0, BLOCKS // G) as i:
                for t in range(G):
                    send_back(i, t)

            for b in range(B):
                seq = slice(T * b * D, T * (b + 1) * D)
                pool.wait_ge(first_added, T * (b + 1))
                pool.wait_ge(second_scaled, T * (b + 1))
                pool.tensor_tensor(x2_sb[:, seq].rearrange("p (t d) -> p t d", t=T), x2_sb[:, seq].rearrange("p (t d) -> p t d", t=T),
                                  back[:, b * T * K * D:(b + 1) * T * K * D].rearrange("p (t k d) -> p t k d", t=T, k=K)[:, :, K - 1, :],
                                  ALU.add).then_inc(both_added, 1)

        @block.scalar
        def _(act):
            def normalize(b, t):
                g = T * b + t
                wait(act, norm_done, 1 if isinstance(g, int) and g in AHEAD[0] else 2)
                wait(act, T1_done, g + 1 - T)
                act.activation(xn[:, t, :], tile(x_sb, b, t), ACT.Identity, bias=norm_at(norm, b, t, 1),
                               scale=norm_at(norm, b, t, 0)).then_inc(xn_done, 1)

            def xnT_out(b, t):
                wait(act, T1_done, T * b + t + 1)
                wait(act, qkv_mm, T * b + t + 1 - T)
                act.activation(xnT[:, t, :], ps_T1, ACT.Identity).then_inc(xnT_done, 1)

            def qT_out(b, t):
                wait(act, qkv_mm, T * b + t + 1)
                wait(act, oT_mm, T * b + t + 1 - T)
                act.activation(qT[:, t, :], ps_qT, ACT.Identity, bias=bq_col[:, 0:1]).then_inc(qT_done, 1)

            def qkv_out(b, t):
                g = T * b + t
                wait(act, qkv_mm, g + 1)
                wait(act, outer_done, g + 1 - T)
                wait(act, prod_done, g + 1 - T)
                wait(act, kv_done, (T - 1) * b)
                act.activation(qkv[:, t, :], ps_qkv, ACT.Identity).then_inc(qkv_done, 1)

            def oT_out(b, t):
                wait(act, oT_mm, T * b + t + 1)
                wait(act, att_mm, T * b + t + 1 - T)
                act.activation(oT[:, t, :], ps_oT, ACT.Identity).then_inc(oT_done, 1)

            def deviation2(b, t):
                wait(act, stats2_done, T * b + t + 1)
                wait(act, rstd2_done, T * b + t + 1 - T)
                act.activation(std2[:, t:t + 1], mv2[:, t, 1:2], ACT.Sqrt, bias=eps[:, 0:1]).then_inc(std2_done, 1)

            def normalize2(b, t):
                wait(act, norm2_done, T * b + t + 1)
                wait(act, x2_done, T * b + t + 1)
                wait(act, T2_done, T * b + t + 1 - T)
                act.activation(xn2[:, t, :], tile(x2_sb, b, t), ACT.Identity, bias=norm_at(norm2, b, t, 1),
                               scale=norm_at(norm2, b, t, 0)).then_inc(xn2_done, 1)

            def rows_out(b, t):
                wait(act, dispatch_done[t], 16 * K * b)
                for k in range(K):
                    act.activation(rows[:, t, k, 0:D], tile(x2_sb, b, t), ACT.Identity, bias=norm_at(norm2, b, t, 1),
                                   scale=norm_at(norm2, b, t, 0)).then_inc(rows_done, 1)

            def xn2T_out(b, t):
                wait(act, T2_done, T * b + t + 1)
                wait(act, lg_mm, T * b + t + 1 - T)
                act.activation(xn2T[:, t, :], ps_T2, ACT.Identity).then_inc(xn2T_done, 1)

            def exponentials(b, t):
                if t == T - 1:
                    wait(act, shift_done, b + 1)
                    wait(act, topi_done, T * b)
                    wait(act, gsum_done, b)
                    act.activation(expd[:, :, :], shifted[:, :, :], ACT.Exp).then_inc(exp_done, 1)

            act.wait_ge(eps_done, 1)
            act.activation(first_root[:, :], eps[:, :], ACT.Sqrt).then_inc(root_done, 1)

            def deviation1(n):
                first, last = AHEAD[n].start, AHEAD[n].stop
                act.wait_ge(stats_done, last)
                act.activation(std[:, first:last], mv[:, first:last, 1], ACT.Sqrt, bias=eps[:, 0:1]).then_inc(std_done, 1)

            deviation1(0)
            act.wait_ge(w_att, 5 * 16)
            run_slots(act, [(11, exponentials), (9, normalize2), (2, qT_out), (2, qkv_out), (1, xnT_out), (15, rows_out), (9, xn2T_out), (7, deviation2), (0, normalize), (5, oT_out)], N, T, at_slot=lambda s: deviation1(1) if s == 2 else None)

            act.wait_ge(table_done, 3)
            act.wait_ge(w_ffn, (3 + HC) * 16)
            at = {}

            def biases_of_group(i):
                at[HIDDEN] = read(mybir.EngineType.Activation, b1_at[0:1, bass.ds(G * i, G)], (E - 1) * HC)

            def xT_out(i, t):
                n = G * i + t
                wait(act, TX_done, n + 1)
                wait(act, h_mm, n + 1 - G)
                act.activation(xT[:, t, :], ps_x[t % 2], ACT.Identity).then_inc(xT_done, 1)

            def hT_out(i, t):
                n = G * i + t
                wait(act, h_mm, n + 1)
                wait(act, y_mm, n + 1 - G)
                for c in range(HC):
                    act.activation(hT[:, t, c, :], ps_h[t % 2][:, c * P:(c + 1) * P], ACT.Relu,
                                   bias=b1_col[:, bass.ds(at[HIDDEN][(t + HIDDEN) % G] + c, 1)]).then_inc(hT_done, 1)

            run_slots(act, [(0, xT_out), (HIDDEN, hT_out)], BLOCKS, G, biases_of_group)

            for b in range(B):
                act.wait_ge(back_in[b], 16)
                for g in range(T * b, T * (b + 1)):
                    at_g = g * K + K - 1
                    act.activation(back[:, at_g * D:(at_g + 1) * D], back[:, at_g * D:(at_g + 1) * D], ACT.Identity,
                                   scale=chosen[:, at_g:at_g + 1]).then_inc(second_scaled, 1)

        @block.vector
        def _(dve):
            def state_out(b, t):
                if t == 0:
                    return
                wait(dve, kv_done, (T - 1) * b + t)
                wait(dve, att_mm, T * b + t - 2)
                wait(dve, oT_mm, T * b + t + 1 - T)
                dve.tensor_tensor(state[:, t, :], ps_state, headmask[:, :], ALU.mult).then_inc(state_done, 1)

            def attend(b, t):
                g = T * b + t
                wait(dve, qkv_done, g + 1)
                wait(dve, run_done, g + 1)
                wait(dve, o_done, g - 1)
                q = qkv[:, t, 0:D].rearrange("p (h a) -> p h a", h=HEADS).unsqueeze(3).to_broadcast([P, HEADS, DH, DH])
                run = ps_run[t % 2].rearrange("p u f -> p (u f)").rearrange("p (h a b) -> p h a b", h=HEADS, a=DH)
                dve.tensor_tensor(prod[:, t % 2, :].rearrange("p (h a b) -> p h a b", h=HEADS, a=DH), run, q,
                                  ALU.mult).then_inc(prod_done, 1)

            def attend_sum(b, t):
                g = T * b + t
                wait(dve, prod_done, g + 1)
                wait(dve, oT_mm, g + 1 - T)
                dve.tensor_reduce(o_sb[:, t, :].rearrange("p (h b) -> p h b", h=HEADS),
                                  prod[:, t % 2, :].rearrange("p (h a b) -> p h b a", h=HEADS, a=DH),
                                  AX_X, ALU.add).then_inc(o_done, 1)

            def add_residual(b, t):
                g = T * b + t
                wait(dve, att_mm, g + 1)
                wait(dve, xb_done, b + 1)
                dve.tensor_tensor(tile(x2_sb, b, t), ps_att, tile(x2_sb, b, t), ALU.add).then_inc(x2_done, 1)

            def stats2_out(b, t):
                g = T * b + t
                wait(dve, x2_done, g + 1)
                apart(dve)
                dve.bn_stats(stats2[:, t, :], tile(x2_sb, b, t)).then_inc(stats2_raw, 1)

            def mean2_out(b, t):
                g = T * b + t
                wait(dve, stats2_raw, g + 1)
                wait(dve, std2_done, g + 1 - T)
                apart(dve)
                dve.bn_aggr(mv2[:, t, :], stats2[:, t, :]).then_inc(stats2_done, 1)

            def scale2_out(b, t):
                g = T * b + t
                wait(dve, std2_done, g + 1)
                dve.reciprocal(norm_at(norm2, b, t, 0), std2[:, t:t + 1]).then_inc(rstd2_done, 1)

            def shift2_out(b, t):
                g = T * b + t
                wait(dve, rstd2_done, g + 1)
                dve.scalar_tensor_tensor(out=norm_at(norm2, b, t, 1), in0=mv2[:, t, 0:1], scalar=-1.0,
                                         in1=norm_at(norm2, b, t, 0), op0=ALU.mult, op1=ALU.mult).then_inc(norm2_done, 1)

            def destinations(b, t):
                wait(dve, dispatch_done[t], 16 * K * b)
                dve.tensor_scalar(rows[:, t, :, D:D + 1].bitcast(I32), dest_in[:, t, :].unsqueeze(2), dest_from[:, bass.ds(b, 1)], None,
                                  ALU.add).then_inc(dest_done, 1)

            def over_e(ap):
                return ap[:, :].unsqueeze(2).to_broadcast([P, T, E])

            def softmax_start(b, t):
                if t < T - 1:
                    return
                wait(dve, lg_mm, T * (b + 1))
                wait(dve, att_mm, T * b + t + 5, N)
                dve.tensor_reduce(gmax[:, :], ps_lg, AX_X, ALU.max).then_inc(gmax_done, 1)
                wait(dve, gmax_done, b + 1)
                dve.tensor_tensor(shifted[:, :, :], ps_lg, over_e(gmax), ALU.subtract).then_inc(shift_done, 1)

            def softmax_end(b, t):
                if t < T - 1:
                    return
                wait(dve, exp_done, b + 1)
                dve.tensor_reduce(gsum[:, :], expd[:, :, :], AX_X, ALU.add).then_inc(gsum_done, 1)
                for u in range(T):
                    dve.max(top[:, u, :], expd[:, u, :]).then_inc(top_done, 1)
                wait(dve, gsum_done, b + 1)
                dve.reciprocal(grec[:, :], gsum[:, :]).then_inc(grec_done, 1)
                for u in range(T):
                    wait(dve, top_done, T * b + u + 1)
                    apart(dve)
                    dve.max_index(top_i[:, u, :], top[:, u, :], expd[:, u, :]).then_inc(topi_done, 1)
                wait(dve, grec_done, b + 1)
                dve.tensor_tensor(chosen[:, bass.ds(T * b * K, T * K)].rearrange("p (t k) -> p t k", t=T), top[:, :, 0:K],
                                  grec[:, :].unsqueeze(2).to_broadcast([P, T, K]), ALU.mult).then_inc(chosen_done, 1)
                wait(dve, topi_done, T * (b + 1))
                dve.tensor_copy(top_f[:, :, :], top_i[:, :, 0:K]).then_inc(topf_done, 1)

            def count(b, t):
                if t < T - 1:
                    return
                wait(dve, topf_done, b + 1)
                dve.tensor_tensor(pick[:, :, :, :], top_f[:, :, :].unsqueeze(3).to_broadcast([P, T, K, E]),
                                  expert_no[:, :].unsqueeze(1).unsqueeze(1).to_broadcast([P, T, K, E]),
                                  ALU.is_equal).then_inc(pick_done, 1)
                wait(dve, pick_done, b + 1)
                wait(dve, place_mm, b)
                dve.tensor_tensor(picked[:, :, :], pick[:, :, 0, :], pick[:, :, 1, :], ALU.add).then_inc(picked_done, 1)

            def places(b, t):
                if t < T - 1:
                    return
                wait(dve, place_mm, b + 1)
                wait(dve, lg_mm, T * b + t + 3, N)
                wait(dve, att_mm, T * b + t + 7, N)
                dve.tensor_tensor(place[:, :, :], ps_place, region_of[:, :].unsqueeze(1).to_broadcast([P, T, E]),
                                  ALU.add).then_inc(place_done, 1)
                dve.tensor_reduce(picked_sum[:, :], picked[:, :, :].rearrange("p t e -> p e t"), AX_X, ALU.add).then_inc(psum_done, 1)
                wait(dve, place_done, b + 1)
                dve.tensor_tensor(place_of[:, :, :, :], pick[:, :, :, :], place[:, :, :].unsqueeze(2).to_broadcast([P, T, K, E]),
                                  ALU.mult).then_inc(placeof_done, 1)
                wait(dve, psum_done, b + 1)
                dve.tensor_tensor(picked_before[:, :], picked_before[:, :], picked_sum[:, :], ALU.add).then_inc(before_done, 1)
                wait(dve, placeof_done, b + 1)
                dve.tensor_reduce(slot_f[:, :, :], place_of[:, :, :, :], AX_X, ALU.add).then_inc(slotf_done, 1)
                wait(dve, before_done, b + 1)
                dve.tensor_copy(picked_before_h[:, :], picked_before[:, :]).then_inc(before_h_done, 1)
                wait(dve, slotf_done, b + 1)
                wait(dve, slots_taken, T // 2 * b)
                dve.tensor_copy(slot_next[:, :].rearrange("p (t k) -> p t k", t=T), slot_f[:, :, :]).then_inc(slot_done, 1)

            def mean1_out(b):
                dve.wait_ge(x_in[b], 16)
                for g in range(b * T, (b + 1) * T):
                    dve.bn_stats(stats[:, g, :], x_sb[:, g * D:(g + 1) * D]).then_inc(stats_raw, 1)
                for g in range(b * T, (b + 1) * T):
                    dve.wait_ge(stats_raw, g + 1)
                    dve.bn_aggr(mv[:, g, :], stats[:, g, :]).then_inc(stats_done, 1)

            def scale1_out(n):
                first, last = AHEAD[n].start, AHEAD[n].stop
                norm_v = norm[:, first * 2:last * 2].rearrange("p (g w) -> p g w", w=2)
                dve.wait_ge(std_done, n + 1)
                dve.reciprocal(norm_v[:, :, 0], std[:, first:last]).then_inc(rstd_done, 1)
                dve.wait_ge(rstd_done, n + 1)
                dve.scalar_tensor_tensor(out=norm_v[:, :, 1], in0=mv[:, first:last, 0], scalar=-1.0, in1=norm_v[:, :, 0],
                                         op0=ALU.mult, op1=ALU.mult).then_inc(norm_done, 1)

            mean1_out(0)

            dve.wait_ge(bias_in, 16)
            dve.wait_ge(parts_cleared, 1)
            dve.tensor_copy(bias_high[:, :], bqkv_bc[:, :]).then_inc(bias_step, 1)
            dve.wait_ge(bias_step, 1)
            dve.tensor_tensor(bias_rest[:, :], bqkv_bc[:, :], bias_high[:, :], ALU.subtract).then_inc(bias_step, 1)
            dve.tensor_copy(bias_parts[0:1, :], bias_high[0:1, :]).then_inc(bias_done, 1)
            dve.wait_ge(bias_step, 2)
            dve.tensor_copy(bias_middle[:, :], bias_rest[:, :]).then_inc(bias_step, 1)
            dve.wait_ge(bias_step, 3)
            dve.tensor_copy(bias_parts[32:33, :], bias_middle[32:33, :]).then_inc(bias_done, 1)
            dve.tensor_tensor(bias_parts[64:65, :], bias_rest[64:65, :], bias_middle[64:65, :], ALU.subtract).then_inc(bias_done, 1)

            scale1_out(0)
            for b in range(1, B):
                mean1_out(b)
            scale1_out(1)
            dve.wait_ge(consts, N_CONSTS)
            run_slots(dve, [(6, scale2_out), (3, attend_sum), (1, state_out), (10, places), (8, softmax_start), (4, add_residual), (6, shift2_out), (9, softmax_end), (12, destinations), (9, count), (4, stats2_out), (2, attend), (4, mean2_out)], N, T)

            steps = 0

            def step(ins):
                nonlocal steps
                steps += 1
                ins.then_inc(table_step, 1)
                dve.wait_ge(table_step, steps)

            dve.wait_ge(cnt_mm, 1)
            dve.tensor_tensor(end_row[:, :], ps_cnt, region_of[0:1, :], ALU.add).then_inc(end_row_done, 1)
            step(dve.tensor_scalar(cnt_i[:, :], ps_cnt, float(P - 1), None, ALU.add))
            step(dve.tensor_scalar(cnt_i[:, :], cnt_i[:, :], P.bit_length() - 1, None, ALU.arith_shift_right))
            step(dve.tensor_copy(n_blocks[:, :], cnt_i[:, :]))
            step(dve.tensor_tensor_scan(end_block[:, :], one_row[:, :], n_blocks[:, :], 0.0, ALU.mult, ALU.add))
            dve.tensor_tensor(past[:, :, :], block_no[:, :].unsqueeze(2).to_broadcast([1, BLOCKS, E]),
                              end_block[:, :].unsqueeze(1).to_broadcast([1, BLOCKS, E]), ALU.is_ge).then_inc(table_step, 1)
            dve.tensor_scalar(jump[:, :], n_blocks[:, :], -float(P), float(REGION), ALU.mult, ALU.add).then_inc(table_step, 1)
            steps += 1
            dve.wait_ge(table_step, steps)
            dve.tensor_reduce(expert_f[:, :], past[:, :, :], AX_X, ALU.add).then_inc(table_step, 1)
            steps += 1
            dve.wait_ge(table_step, steps)
            dve.tensor_tensor(skipped[:, :, :], past[:, :, :], jump[:, :].unsqueeze(1).to_broadcast([1, BLOCKS, E]),
                              ALU.mult).then_inc(table_step, 1)
            steps += 1
            dve.wait_ge(table_step, steps)
            dve.tensor_scalar(w1_at[:, 0:BLOCKS], expert_f[:, :], float(E - 1), float(H), ALU.min, ALU.mult).then_inc(table_done, 1)
            dve.tensor_scalar(b1_at[:, HIDDEN:HIDDEN + BLOCKS], expert_f[:, :], float(E - 1), float(HC), ALU.min, ALU.mult).then_inc(table_done, 1)
            dve.tensor_scalar(w2_at[:, OUTPUT:OUTPUT + BLOCKS], expert_f[:, :], float(E - 1), float(D), ALU.min, ALU.mult).then_inc(table_done, 1)
            steps += 1
            dve.wait_ge(table_step, steps)
            step(dve.tensor_reduce(row_f[:, :], skipped[:, :, :], AX_X, ALU.add))
            step(dve.tensor_tensor(row_f[:, :], row_f[:, :], block_row[:, :], ALU.add))
            dve.tensor_scalar(row_at[:, :], row_f[:, :], float(PAD_BLOCK), None, ALU.min).then_inc(table_done, 1)

            dve.wait_ge(table_done, 3)
            dve.wait_ge(w_ffn, (3 + HC) * 16)

            at = {}

            def experts_of_group(i):
                at[0] = read(mybir.EngineType.DVE, w1_at[0:1, bass.ds(G * i, G)], (E - 1) * H)
                at[OUTPUT] = read(mybir.EngineType.DVE, w2_at[0:1, bass.ds(G * i, G)], (E - 1) * D)

            def w1_out(i, t):
                wait(dve, h_mm, G * i + t + 1 - W)
                dve.tensor_copy(w1_of[:, t % W, :], w1_sb[:, bass.ds(at[0][t], H)]).then_inc(w1_done, 1)

            def y_out(i, t):
                n = G * i + t
                wait(dve, y_mm, n + 1)
                wait(dve, return_done[t], 16 * i)
                dve.tensor_tensor(y_sb[:, t, :], ps_y[t % 2], b2_bc[:, bass.ds(at[OUTPUT][(t + OUTPUT) % G], D)], ALU.add).then_inc(y_done, 1)

            run_slots(dve, [(0, w1_out), (OUTPUT, y_out)], BLOCKS, G, experts_of_group)

            for b in range(B):
                dve.wait_ge(back_in[b], 16)
                for g in range(T * b, T * (b + 1)):
                    dst = x2_sb[:, g * D:(g + 1) * D]
                    dve.scalar_tensor_tensor(out=dst, in0=back[:, g * K * D:(g * K + 1) * D], scalar=chosen[:, g * K:g * K + 1],
                                             in1=dst, op0=ALU.mult, op1=ALU.add).then_inc(first_added, 1)

        @block.tensor
        def _(pe):
            def transpose1(b, t):
                g = T * b + t
                wait(pe, xn_done, g + 1)
                wait(pe, oT_done, g - 4)
                pe.transpose(ps_T1, xn[:, t, :], ident[:, :]).then_inc(T1_done, 1)

            def project(b, t):
                g = T * b + t
                wait(pe, xnT_done, g + 1)
                wait(pe, bias_done, 3)
                wait(pe, xn2T_done, g - 7)
                wait(pe, qkv_done, g)
                pe.matmul(ps_qT, wqkv_sb[:, 0:D], xnT[:, t, :], start=True, stop=True)
                pe.matmul(ps_qkv, xnT[:, t, :], wqkv_sb[:, :], start=True, stop=False)
                pe.matmul(ps_qkv, ones[:, :], bias_parts[:, :], start=False, stop=True).then_inc(qkv_mm, 1)

            def running_sums(b, t):
                g = T * b + t
                wait(pe, outer_done, g + 1)
                wait(pe, prod_done, g - 1)
                for u in range(2):
                    mm = pe.matmul(ps_run[t % 2][:, u, :], causal[:, :], outer[:, t, 512 * u:512 * (u + 1)],
                                   start=True, stop=True)
                mm.then_inc(run_done, 1)

            def sum_state(b, t):
                if t == 0:
                    return
                wait(pe, qkv_done, T * b + t)
                wait(pe, state_done, (T - 1) * b + t - 1)
                wait(pe, x2_done, T * b + t - 3)
                for u in range(t):
                    mm = pe.matmul(ps_state, qkv[:, u, D:2 * D], qkv[:, u, 2 * D:3 * D], start=(u == 0), stop=(u == t - 1))
                mm.then_inc(kv_done, 1)

            def o_transposed(b, t):
                g = T * b + t
                wait(pe, o_done, g + 1)
                wait(pe, xnT_done, g + 5, N)
                wait(pe, oT_done, g)
                mm = pe.matmul(ps_oT, o_sb[:, t, :], ident[:, :], start=True, stop=(t == 0))
                if t:
                    wait(pe, state_done, (T - 1) * b + t)
                    wait(pe, qT_done, g + 1)
                    mm = pe.matmul(ps_oT, state[:, t, :], qT[:, t, :], start=False, stop=True)
                mm.then_inc(oT_mm, 1)

            def project_out(b, t):
                g = T * b + t
                wait(pe, oT_done, g + 1)
                wait(pe, x2_done, g)
                wait(pe, state_done, (T - 1) * b + min(t + 2, T - 1) + (t == T - 1), (T - 1) * B)
                pe.matmul(ps_att, oT[:, t, :], wo_sb[:, :], start=True, stop=True).then_inc(att_mm, 1)

            def transpose2(b, t):
                g = T * b + t
                wait(pe, xn2_done, g + 1)
                wait(pe, qT_done, g + 8, N)
                wait(pe, xn2T_done, g)
                pe.transpose(ps_T2, xn2[:, t, :], ident[:, :]).then_inc(T2_done, 1)

            def gate(b, t):
                wait(pe, xn2T_done, T * b + t + 1)
                wait(pe, x2_done, T * b + t + 4, N)
                if t == 0:
                    wait(pe, shift_done, b)
                if t == 2:
                    wait(pe, place_done, b)
                pe.matmul(ps_lg[:, t, :], xn2T[:, t, :], wg_sb[:, :], start=True, stop=True).then_inc(lg_mm, 1)

            def rank(b, t):
                if t < T - 1:
                    return
                wait(pe, picked_done, b + 1)
                wait(pe, x2_done, T * b + t + 6, N)
                wait(pe, before_h_done, b)
                pe.matmul(ps_place, earlier[:, :], picked[:, :, :], start=True, stop=False, skip_group_check=True)
                for u in range(T - 1):
                    pe.matmul(ps_place[:, u + 1:T, :], ones[:, :],
                              picked[:, u, :].unsqueeze(1).to_broadcast([P, T - 1 - u, E]),
                              start=False, stop=False, skip_group_check=True)
                mm = pe.matmul(ps_place, ones[:, :], picked_before_h[:, :].unsqueeze(1).to_broadcast([P, T, E]),
                               start=False, stop=True, skip_group_check=True)
                mm.then_inc(place_mm, 1)

            pe.wait_ge(consts, N_CONSTS)
            pe.wait_ge(w_att, 5 * 16)
            run_slots(pe, [(1, project), (0, transpose1), (2, sum_state), (11, rank), (9, gate), (5, project_out), (8, transpose2), (3, running_sums), (4, o_transposed)], N, T)

            pe.wait_ge(before_h_done, B)
            pe.matmul(ps_cnt, ones[:, 0:1], picked_before_h[:, :], start=True, stop=True).then_inc(cnt_mm, 1)

            pe.wait_ge(table_done, 3)
            pe.wait_ge(w_ffn, (3 + HC) * 16)

            at = {}

            def experts_of_group(i):
                at[OUTPUT] = read(mybir.EngineType.PE, w2_at[0:1, bass.ds(G * i, G)], (E - 1) * D)

            def transpose_x(i, t):
                n = G * i + t
                pe.wait_ge(xt_in[t], 16 * (i + 1))
                wait(pe, xT_done, n - 1)
                pe.transpose(ps_x[t % 2], xt[:, t, 0:D], ident[:, :]).then_inc(TX_done, 1)

            def hidden(i, t):
                n = G * i + t
                wait(pe, xT_done, n + 1)
                wait(pe, w1_done, n + 1)
                wait(pe, hT_done, HC * (n - 1))
                for c in range(HC):
                    mm = pe.matmul(ps_h[t % 2][:, c * P:(c + 1) * P], w1_of[:, t % W, c * P:(c + 1) * P], xT[:, t, :],
                                   start=True, stop=True)
                mm.then_inc(h_mm, 1)

            def output(i, t):
                n = G * i + t
                wait(pe, hT_done, HC * (n + 1))
                wait(pe, y_done, n - 1)
                for c in range(HC):
                    mm = pe.matmul(ps_y[t % 2], hT[:, t, c, :], w2_sb[:, c, bass.ds(at[OUTPUT][(t + OUTPUT) % G], D)], start=(c == 0), stop=(c == HC - 1))
                mm.then_inc(y_mm, 1)

            run_slots(pe, [(0, transpose_x), (HIDDEN, hidden), (OUTPUT, output)], BLOCKS, G, experts_of_group)


_OUT = (8, 512, 128)


def kernel(L0_attn_x, L0_attn_wq_w, L0_attn_wq_b, L0_attn_wk_w, L0_attn_wk_b, L0_attn_wv_w, L0_attn_wv_b,
           L0_attn_wo_w, L0_attn_wo_b, L0_ffn_Wg, L0_ffn_W1, L0_ffn_b1, L0_ffn_W2, L0_ffn_b2):
    import numpy as np
    import concourse.bacc as bacc
    from concourse.bass_utils import run_bass_kernel_spmd

    arrays = {
        "x": L0_attn_x,
        "w_qkv": np.concatenate([np.asarray(w).T for w in (L0_attn_wq_w, L0_attn_wk_w, L0_attn_wv_w)], axis=1),
        "b_qkv": np.concatenate([np.asarray(b) for b in (L0_attn_wq_b, L0_attn_wk_b, L0_attn_wv_b)]),
        "b_q": np.asarray(L0_attn_wq_b).reshape(-1, 1),
        "w_o": np.asarray(L0_attn_wo_w).T,
        "b_o": L0_attn_wo_b,
        "w_gate": L0_ffn_Wg,
        "w1": L0_ffn_W1,
        "b1": np.asarray(L0_ffn_b1).reshape(-1, 128).T,
        "w2": L0_ffn_W2,
        "b2": np.asarray(L0_ffn_b2).reshape(-1),
    }
    arrays = {name: np.ascontiguousarray(a) for name, a in arrays.items()}
    nc = bacc.Bacc("TRN2", target_bir_lowering=False, num_devices=1)
    args = {name: nc.dram_tensor(name, a.shape, mybir.dt.from_np(a.dtype), kind="ExternalInput").ap()
            for name, a in arrays.items()}
    out = nc.dram_tensor("out", _OUT, F32, kind="ExternalOutput").ap()
    preln_linear_attention_moe(nc, out=out, **args)
    result = run_bass_kernel_spmd(nc, [arrays], core_ids=[0])
    return result.results[0]["out"]
```
